# Optimizing a Trainium2 kernel written in Bass

```python
import numpy as np
import jax
import jax.numpy as jnp

def _softmax(x, axis=-1):
    return jax.nn.softmax(x, axis=axis)

def _gelu(x):
    return jax.nn.gelu(x, approximate=True)

def _silu(x):
    return jax.nn.silu(x)

def _sigmoid(x):
    return jax.nn.sigmoid(x)

def _layernorm(x, axis=-1, eps=1e-05):
    m = jnp.mean(x, axis=axis, keepdims=True)
    v = jnp.var(x, axis=axis, keepdims=True)
    return (x - m) / jnp.sqrt(v + eps)

def _scatter_add(tgt, idx, src, axis=0):
    return tgt.at[idx].add(src)

def _segment_sum(src, seg, n):
    return jax.ops.segment_sum(src, seg, n)
kernel_name = 'mk_xattn_ffn_d1_seqx_r8_5c5219'

def setup_inputs(seed: int=0):
    np.random.seed(seed)
    _w = jnp.asarray

    def _rec_inputs():
        import jax
        import jax.numpy as jnp
        _rk = jax.random.key(seed)
        x = -0.0005207 + 1.001 * jax.random.normal(jax.random.fold_in(_rk, 1), (1, 1024, 128), jnp.float32)
        _lenS = 1024 - jax.random.randint(jax.random.fold_in(_rk, 7), (1,), 0, max(1, 1024 // 4) + 1, jnp.int32)
        _lenS2 = 6404 - jax.random.randint(jax.random.fold_in(_rk, 8), (1,), 0, max(1, 6404 // 4) + 1, jnp.int32)
        _ctx_1024P = jax.random.normal(jax.random.fold_in(_rk, 11), (1, 16, 128), jnp.float32)
        _ctx_1024c = jax.random.dirichlet(jax.random.fold_in(_rk, 511), 0.3 * jnp.ones((16,), jnp.float32), (1, 6404))
        _ctx_1024t = jnp.einsum('bsk,bkd->bsd', _ctx_1024c, _ctx_1024P)
        _ctx_1024t = _ctx_1024t * jax.lax.rsqrt(jnp.mean(jnp.square(_ctx_1024t)) + 1e-12) * 0.953939
        ctx_1024 = -1.39393e-06 + 0.999914 * (_ctx_1024t + 0.3 * jax.random.normal(jax.random.fold_in(_rk, 611), (1, 6404, 128), jnp.float32))
        _validS = jnp.arange(1024)[None, :] < _lenS[:, None]
        _validS2 = jnp.arange(6404)[None, :] < _lenS2[:, None]
        _causal = jnp.tril(jnp.ones((1024, 1024), dtype=bool))
        mask_BxS2_bf1 = jnp.ones((1, 6404), dtype=bool)
        return (x, ctx_1024, mask_BxS2_bf1)
    x, ctx_1024, mask_BxS2_bf1 = _rec_inputs()

    def _L0_xattn_setup():
        import jax, jax.numpy as jnp
        import numpy as np
        B, M, N = (2, 128, 256)
        D_MODEL = 128
        H, HKV, D = (16, 4, 64)
        GROUPS = H // HKV
        THETA = 10000.0
        MAX_REL = M + N

        def _freqs_cis(dim, seq_len, theta):
            inv = 1.0 / theta ** (jnp.arange(0, dim, 2, dtype=jnp.float32) / dim)
            f = jnp.outer(jnp.arange(seq_len, dtype=jnp.float32), inv)
            f = jnp.repeat(f, 2, axis=-1)
            return (jnp.cos(f), jnp.sin(f))

        def _apply_rope(x, cos, sin):
            cos = cos[None, None]
            sin = sin[None, None]
            d = x.shape[-1]
            x1, x2 = (x[..., :d // 2], x[..., d // 2:])
            c1, c2 = (cos[..., :d // 2], cos[..., d // 2:])
            s1, s2 = (sin[..., :d // 2], sin[..., d // 2:])
            return jnp.concatenate([x1 * c1 - x2 * s1, x1 * s2 + x2 * c2], axis=-1)
        key = jax.random.key(seed)
        ks = jax.random.split(key, 8)
        sc = lambda fan_in: 1.0 / np.sqrt(fan_in)
        return {'q': jax.random.normal(ks[0], (B, M, D_MODEL), jnp.float32), 'kv': jax.random.normal(ks[1], (B, N, D_MODEL), jnp.float32), 'Wq': jax.random.normal(ks[2], (D_MODEL, H * D), jnp.float32) * sc(D_MODEL), 'Wk': jax.random.normal(ks[3], (D_MODEL, HKV * D), jnp.float32) * sc(D_MODEL), 'Wv': jax.random.normal(ks[4], (D_MODEL, HKV * D), jnp.float32) * sc(D_MODEL), 'Wo': jax.random.normal(ks[5], (H * D, D_MODEL), jnp.float32) * sc(H * D), 'rel_pos_bias': jnp.zeros((H, MAX_REL), jnp.float32), 'mask': jnp.ones((B, N), dtype=bool)}
    _L0_xattn_all = _L0_xattn_setup()
    _L0_xattn_in = {k: v for k, v in _L0_xattn_all.items() if k in ('Wq', 'Wk', 'Wv', 'Wo', 'rel_pos_bias')}
    del _L0_xattn_all

    def _L0_ffn_setup():
        import jax, jax.numpy as jnp
        import numpy as np
        D_MODEL = 128
        key = jax.random.key(seed)
        k_x, k_w, k_a1, k_a2 = jax.random.split(key, 4)
        x = jax.random.normal(k_x, (4, 256, D_MODEL), dtype=jnp.float32)
        weight = jax.random.normal(k_w, (D_MODEL, D_MODEL), dtype=jnp.float32) * 0.02
        aux_weight1 = jax.random.normal(k_a1, (D_MODEL, D_MODEL), dtype=jnp.float32) * 0.02
        aux_weight2 = jax.random.normal(k_a2, (D_MODEL, D_MODEL), dtype=jnp.float32) * 0.02
        bias = jnp.zeros((D_MODEL,), dtype=jnp.float32)
        return {'x': x, 'weight': weight, 'aux_weight1': aux_weight1, 'aux_weight2': aux_weight2, 'bias': bias}
    _L0_ffn_all = _L0_ffn_setup()
    _L0_ffn_in = {k: v for k, v in _L0_ffn_all.items() if k in ('weight', 'aux_weight1', 'aux_weight2', 'bias')}
    del _L0_ffn_all
    return {'x': x, 'ctx_1024': ctx_1024, 'mask_BxS2_bf1': mask_BxS2_bf1, 'L0_xattn_Wq': _L0_xattn_in['Wq'], 'L0_xattn_Wk': _L0_xattn_in['Wk'], 'L0_xattn_Wv': _L0_xattn_in['Wv'], 'L0_xattn_Wo': _L0_xattn_in['Wo'], 'L0_xattn_rel_pos_bias': _L0_xattn_in['rel_pos_bias'], 'L0_ffn_weight': _L0_ffn_in['weight'], 'L0_ffn_aux_weight1': _L0_ffn_in['aux_weight1'], 'L0_ffn_aux_weight2': _L0_ffn_in['aux_weight2'], 'L0_ffn_bias': _L0_ffn_in['bias']}

def reference(x, ctx_1024, mask_BxS2_bf1, L0_xattn_Wq, L0_xattn_Wk, L0_xattn_Wv, L0_xattn_Wo, L0_xattn_rel_pos_bias, L0_ffn_weight, L0_ffn_aux_weight1, L0_ffn_aux_weight2, L0_ffn_bias):
    import jax
    import jax.numpy as jnp

    def _L0_xattn_ref(q, kv, Wq, Wk, Wv, Wo, rel_pos_bias, mask):
        import jax, jax.numpy as jnp
        import numpy as np
        B, M, N = (2, 128, 256)
        D_MODEL = 128
        H, HKV, D = (16, 4, 64)
        GROUPS = H // HKV
        THETA = 10000.0
        MAX_REL = M + N

        def _freqs_cis(dim, seq_len, theta):
            inv = 1.0 / theta ** (jnp.arange(0, dim, 2, dtype=jnp.float32) / dim)
            f = jnp.outer(jnp.arange(seq_len, dtype=jnp.float32), inv)
            f = jnp.repeat(f, 2, axis=-1)
            return (jnp.cos(f), jnp.sin(f))

        def _apply_rope(x, cos, sin):
            cos = cos[None, None]
            sin = sin[None, None]
            d = x.shape[-1]
            x1, x2 = (x[..., :d // 2], x[..., d // 2:])
            c1, c2 = (cos[..., :d // 2], cos[..., d // 2:])
            s1, s2 = (sin[..., :d // 2], sin[..., d // 2:])
            return jnp.concatenate([x1 * c1 - x2 * s1, x1 * s2 + x2 * c2], axis=-1)
        Bq, Mq, _ = q.shape
        Nk = kv.shape[1]
        Q = (q @ Wq).reshape(Bq, Mq, H, D).transpose(0, 2, 1, 3)
        K = (kv @ Wk).reshape(Bq, Nk, HKV, D).transpose(0, 2, 1, 3)
        V = (kv @ Wv).reshape(Bq, Nk, HKV, D).transpose(0, 2, 1, 3)
        cos_q, sin_q = _freqs_cis(D, Mq, THETA)
        cos_k, sin_k = _freqs_cis(D, Nk, THETA)
        Q = _apply_rope(Q, cos_q, sin_q)
        K = _apply_rope(K, cos_k, sin_k)
        K = jnp.repeat(K, GROUPS, axis=1)
        V = jnp.repeat(V, GROUPS, axis=1)
        scale = D ** (-0.5)
        scores = jnp.einsum('bhqd,bhkd->bhqk', Q, K) * scale
        rel = jnp.abs(jnp.arange(Mq)[:, None] - jnp.arange(Nk)[None, :])
        rel = jnp.clip(rel, 0, MAX_REL - 1)
        scores = scores + rel_pos_bias[:, rel][None]
        m = mask[:, None, None, :]
        scores = jnp.where(m, scores, -1000000000.0)
        attn = jax.nn.softmax(scores, axis=-1)
        out = jnp.einsum('bhqk,bhkd->bhqd', attn, V)
        out = out.transpose(0, 2, 1, 3).reshape(Bq, Mq, H * D)
        return out @ Wo

    def _L0_ffn_ref(x, weight, aux_weight1, aux_weight2, bias):
        import jax, jax.numpy as jnp
        import numpy as np
        D_MODEL = 128
        h = jnp.einsum('btc,cd->btd', x, weight)
        h = jnp.einsum('btc,cd->btd', h, aux_weight1)
        h = jnp.einsum('btc,cd->btd', h, aux_weight2)
        return jnp.tanh(h + bias)
    x = x + _L0_xattn_ref(_layernorm(x, axis=-1), ctx_1024, L0_xattn_Wq, L0_xattn_Wk, L0_xattn_Wv, L0_xattn_Wo, L0_xattn_rel_pos_bias, mask_BxS2_bf1)
    x = x + _L0_ffn_ref(_layernorm(x, axis=-1), L0_ffn_weight, L0_ffn_aux_weight1, L0_ffn_aux_weight2, L0_ffn_bias)
    return x

_drawn_inputs = setup_inputs


def setup_inputs(seed=0):
    import zlib

    import numpy as np

    out = dict(_drawn_inputs(seed))
    spreads = {'L0_xattn_rel_pos_bias': (0.0, 2.0), 'L0_ffn_bias': (0.0, 0.1)}
    factors = {'L0_ffn_weight': 5.647, 'L0_ffn_aux_weight1': 5.735, 'L0_ffn_aux_weight2': 5.625}
    for name, (base, spread) in spreads.items():
        noise = np.random.default_rng([zlib.crc32(name.encode()), seed]).standard_normal(out[name].shape)
        drawn = base * np.exp(spread * noise) if base else spread * noise
        out[name] = jnp.asarray(drawn.astype(out[name].dtype))
    for name, factor in factors.items():
        out[name] = (out[name] * factor).astype(out[name].dtype)
    return out
```

```python
from contextlib import ExitStack

import concourse.bass as bass
from concourse import mybir

ALU = mybir.AluOpType
ACT = mybir.ActivationFunctionType
AX = mybir.AxisListType
F32 = mybir.dt.float32
F32R = mybir.dt.float32r
BF16 = mybir.dt.bfloat16
U8 = mybir.dt.uint8

P = 128
ROWS = 1024
KEYS = 6404
DM = 128
HEADS = 16
GROUPS = 4
REP = HEADS // GROUPS
D = 64
CLIP = 383
CHUNK = 512
CHUNKS = -(-KEYS // CHUNK)
KEYS_PAD = CHUNKS * CHUNK
PAD_TILES = KEYS_PAD // 128 - KEYS // 128
TILES = -(-KEYS // P)
UNIT = 512
HALVES = ROWS // UNIT
BLOCKS = UNIT // P
VCOLS = 3 * D + 1
VLO = 2 * D + 1
ONES = 2 * D
MASKED = -1.0e9
PEN = float(2 ** 30)
ROW_NEGMAX_HI, ROW_PEN, ROW_NEGMAX_LO = 64, 65, 96
EPS = 1e-5

PIECE = 1024
PIECES = -(-KEYS // PIECE)
PIECE_TILES = PIECE // P
SEEKS = BLOCKS * PIECES
TABLE = 2 * PIECE + UNIT - P
S_BUFS = 4
LAG = 2


def piece_width(c):
    return min(PIECE, KEYS - c * PIECE)


def biased_piece(half, c):
    return c == 0 or (c == 1 and half == 0)


def biased_tile(half, t):
    low = t * P + half * UNIT
    return low + P - 1 + UNIT - 1 > ROWS - 1 - CLIP and low < ROWS - 1 + CLIP


BAND = [[t for t in range(TILES) if biased_tile(u, t)] for u in range(HALVES)]
BAND_PER_HEAD = sum(map(len, BAND))
ADDS = [BLOCKS * sum(biased_piece(u, c) for c in range(PIECES)) for u in range(HALVES)]
COPIES = [SEEKS - n for n in ADDS]
FOLDS = BLOCKS * (PIECES - 1)

SEEK_STEP = [k * 39 // SEEKS for k in range(SEEKS)]
SEEK_AT = {}
for _k, _s in enumerate(SEEK_STEP):
    SEEK_AT.setdefault(_s, []).append(_k)
FOLD_STEP, SPLIT_STEP, ROWMAX_STEP = 40, 44, 47


def attention(nc, ins, out):
    outer = ExitStack()
    with outer:
        def dram(name, shape, dt):
            return nc.dram_tensor(name, shape, dt, kind="Internal").ap()

        k_scr = dram("k_scr", [GROUPS, P, KEYS_PAD], F32)
        q_scr = dram("q_scr", [HEADS, P, ROWS], F32)
        v_scr = dram("v_scr", [GROUPS, P, KEYS_PAD // P * VCOLS], BF16)

        mask_scr = dram("mask_scr", [1, KEYS_PAD], F32)

        project(nc, ins, k_scr, q_scr, v_scr, mask_scr)
        attn = outer.enter_context(nc.sbuf_tensor("attn", [P, ROWS // P, HEADS * D], F32))
        attend(nc, ins, k_scr, q_scr, v_scr, attn)
        finish(nc, ins, attn, out)


def layer_norm(dve, act, x, xc, sq, st, s_dve, s_act, base_dve, base_act, factor, role):
    mean, var, sd, rs = (st[:, i, :] for i in range(4))
    wide = x.shape
    if role == "act":
        act.wait_ge(s_dve, base_dve + 6)
        act.activation(sd, var, ACT.Sqrt).then_inc(s_act, 1)
        return
    dve.tensor_reduce(mean, x, AX.X, ALU.add).then_inc(s_dve, 1)
    dve.wait_ge(s_dve, base_dve + 1)
    dve.tensor_scalar(mean, mean, -1.0 / DM, None, ALU.mult).then_inc(s_dve, 1)
    dve.wait_ge(s_dve, base_dve + 2)
    dve.tensor_tensor(xc, x, mean.unsqueeze(2).to_broadcast(wide), ALU.add).then_inc(s_dve, 1)
    dve.wait_ge(s_dve, base_dve + 3)
    dve.tensor_tensor(sq, xc, xc, ALU.mult).then_inc(s_dve, 1)
    dve.wait_ge(s_dve, base_dve + 4)
    dve.tensor_reduce(var, sq, AX.X, ALU.add).then_inc(s_dve, 1)
    dve.wait_ge(s_dve, base_dve + 5)
    dve.tensor_scalar(var, var, 1.0 / DM, EPS, ALU.mult, ALU.add).then_inc(s_dve, 1)
    dve.wait_ge(s_act, base_act + 1)
    dve.reciprocal(rs, sd).then_inc(s_dve, 1)
    dve.wait_ge(s_dve, base_dve + 7)
    dve.tensor_scalar(rs, rs, factor, None, ALU.mult).then_inc(s_dve, 1)
    dve.wait_ge(s_dve, base_dve + 8)
    dve.tensor_tensor(xc, xc, rs.unsqueeze(2).to_broadcast(wide), ALU.mult).then_inc(s_dve, 1)


def project(nc, ins, k_scr, q_scr, v_scr, mask_scr):
    with ExitStack() as ctx:
        def sb(name, shape, dt):
            return ctx.enter_context(nc.sbuf_tensor(name, shape, dt))

        def sem(name):
            return ctx.enter_context(nc.semaphore(name))

        x = sb("x", [P, ROWS // P, DM], F32)
        xc = sb("xc", [P, ROWS // P, DM], F32)
        sq = sb("sq", [P, ROWS // P, DM], F32)
        st = sb("st", [P, 4, ROWS // P], F32)
        xT = sb("xT", [DM, ROWS], F32)
        ident = sb("ident", [P, P], F32)
        wk = sb("wk", [DM, GROUPS, 2, P], F32)
        wv = sb("wv", [DM, GROUPS * D], F32)
        wq = sb("wq", [DM, 2, 2, 2, P], F32)
        cos_q = sb("cos_q", [P, ROWS], F32)
        sin_q = sb("sin_q", [P, ROWS], F32)
        valid = sb("valid", [P, PAD_TILES], F32)
        ctxT = sb("ctxT", [DM, 2, CHUNK], F32)
        cos_k = sb("cos_k", [P, 2, CHUNK], F32)
        sin_k = sb("sin_k", [P, 2, CHUNK], F32)
        maskf = sb("maskf", [P, 2, CHUNK], F32)
        t_cos = sb("t_cos", [P, 2, CHUNK], F32)
        t_sin = sb("t_sin", [P, 2, CHUNK], F32)
        rot = sb("rot", [P, 4, CHUNK], F32)
        parts = sb("parts", [P, 4, CHUNK], F32R)
        vst = sb("vst", [P, 2, GROUPS, 4, VCOLS], BF16)
        vrest = sb("vrest", [P, 2, GROUPS, D], F32)

        plain_ps = ctx.enter_context(nc.psum_tensor("plain_ps", [P, 2, 512], F32))
        swap_ps = ctx.enter_context(nc.psum_tensor("swap_ps", [P, 2, 512], F32))
        v_ps = ctx.enter_context(nc.psum_tensor("v_ps", [P, 2, 512], F32))
        x_ps = ctx.enter_context(nc.psum_tensor("x_ps", [P, 2, 4, P], F32))

        s_x = sem("p_x")
        s_const = sem("p_const")
        s_chunk = [sem("p_chunk0"), sem("p_chunk1")]
        s_wq = [sem("p_wq0"), sem("p_wq1")]
        s_ln = sem("p_ln")
        s_sqrt = sem("p_sqrt")
        s_xT = sem("p_xT")
        s_xTs = sem("p_xTs")
        s_maskf = sem("p_maskf")
        s_masked = sem("p_masked")
        s_proj = sem("p_proj")
        s_terms = sem("p_terms")
        s_rot = sem("p_rot")
        s_hi = sem("p_hi")
        s_lo = sem("p_lo")
        s_out = sem("p_out")
        s_v = sem("p_v")
        s_vh = sem("p_vh")
        s_vr = sem("p_vr")
        s_vm = sem("p_vm")
        s_vl = sem("p_vl")
        s_ones = sem("p_ones")
        s_vout = sem("p_vout")

        v_dst = v_scr.rearrange("g p (t n) -> p g (t n)", n=VCOLS)

        def load_chunk(sp, c, b, used):
            cols = bass.ds(c * CHUNK, CHUNK)
            if used is not None:
                sp.wait_ge(s_v, 4 * (used + 1))
                sp.wait_ge(s_terms, 4 * (used + 1))
            sp.dma_start(ctxT[:, b, :], ins["ctxT"][:, cols]).then_inc(s_chunk[b], 16)
            for half in range(2):
                rows = slice(half * D, (half + 1) * D)
                sp.dma_start(cos_k[rows, b, :], ins["cos_k"][:, cols]).then_inc(s_chunk[b], 16)
                sp.dma_start(sin_k[rows, b, :], ins["sin_k"][:, cols]).then_inc(s_chunk[b], 16)
            sp.dma_start(maskf[:, b, :], mask_scr[:, cols].to_broadcast([P, CHUNK])
                         ).then_inc(s_chunk[b], 16)

        def store_keys(sp, c, b):
            for g in range(GROUPS):
                sp.wait_ge(s_lo, 4 * c + g + 1)
                sp.dma_start(k_scr[g, :, bass.ds(c * CHUNK, CHUNK)], parts[:, g, :].bitcast(F32)
                             ).then_inc(s_out, 16)
            sp.wait_ge(s_vl, 4 * (c + 1))
            sp.wait_ge(s_ones, 2 if c is CHUNKS - 1 else 1)
            sp.dma_start(v_dst[:, :, bass.ds(c * 4 * VCOLS, 4 * VCOLS)],
                         vst[:, b].rearrange("p g t n -> p g (t n)")).then_inc(s_vout, 16)

        def load_wq(sp, pair, b, used):
            if used:
                sp.wait_ge(s_proj, 4 * CHUNKS + 4 * (pair - 1))
            sp.dma_start(wq[:, b], ins["wq"][:, bass.ds(pair * 2, 2)]).then_inc(s_wq[b], 16)

        def store_queries(sp, pair):
            for i in range(4):
                sp.wait_ge(s_lo, 4 * (CHUNKS + pair) + i + 1)
                sp.dma_start(q_scr[pair * 2 + i // 2, :, (i % 2) * UNIT:(i % 2 + 1) * UNIT],
                             parts[:, i, :].bitcast(F32)).then_inc(s_out, 16)

        pairs = CHUNKS // 2
        block = ctx.enter_context(nc.Block())

        @block.sync
        def _(sp):
            sp.dma_start(wk[:, :, :, :], ins["wk"]).then_inc(s_const, 16)
            sp.wait_ge(s_maskf, 16)
            load_chunk(sp, 0, 0, None)
            sp.dma_start(x[:, :, :], ins["x"]).then_inc(s_x, 16)
            sp.dma_start(ident[:, :], ins["ident"]).then_inc(s_x, 16)
            sp.dma_start(wv[:, :], ins["wv"]).then_inc(s_const, 16)
            sp.dma_start(valid[:, :], ins["valid"]).then_inc(s_const, 16)
            for half in range(2):
                rows = slice(half * D, (half + 1) * D)
                sp.dma_start(cos_q[rows, :], ins["cos_q"]).then_inc(s_const, 16)
                sp.dma_start(sin_q[rows, :], ins["sin_q"]).then_inc(s_const, 16)
            load_chunk(sp, 1, 1, None)
            load_wq(sp, 0, 0, False)
            load_wq(sp, 1, 1, False)
            with sp.Fori(0, pairs - 1) as i:
                for b in range(2):
                    store_keys(sp, i * 2 + b, b)
                    load_chunk(sp, i * 2 + b + 2, b, i * 2 + b)
            store_keys(sp, CHUNKS - 3, 0)
            load_chunk(sp, CHUNKS - 1, 0, CHUNKS - 3)
            store_keys(sp, CHUNKS - 2, 1)
            store_keys(sp, CHUNKS - 1, 0)
            with sp.Fori(0, HEADS // 4 - 1) as i:
                for b in range(2):
                    store_queries(sp, i * 2 + b)
                    load_wq(sp, i * 2 + b + 2, b, True)
            store_queries(sp, HEADS // 2 - 2)
            store_queries(sp, HEADS // 2 - 1)
            sp.wait_ge(s_out, 16 * 4 * (CHUNKS + HEADS // 2))
            sp.wait_ge(s_vout, 16 * CHUNKS)

        def free_after(n4, i, sem_, eng):
            eng.wait_ge(sem_, n4 + max(i - 1, 0))

        def through_chunks(eng, chunk):
            with eng.Fori(0, pairs) as i:
                chunk(i * 2, 0, i)
                chunk(i * 2 + 1, 1, i)
            chunk(CHUNKS - 1, 0, pairs)

        def through_pairs(eng, pair):
            with eng.Fori(0, HEADS // 4) as i:
                pair(i * 2, 0, i)
                pair(i * 2 + 1, 1, i)

        @block.tensor
        def _(pe):
            def project_item(n4, i, w_plain, w_swap, rhs):
                free_after(n4, i, s_terms, pe)
                pe.matmul(plain_ps[:, i % 2, :], w_plain, rhs, start=True, stop=True)
                pe.matmul(swap_ps[:, i % 2, :], w_swap, rhs, start=True, stop=True).then_inc(s_proj, 1)

            def chunk(c, b, i):
                pe.wait_ge(s_chunk[b], 96 * (i + 1))
                for g in range(GROUPS):
                    project_item(c * 4, g, wk[:, g, 0, :], wk[:, g, 1, :], ctxT[:, b, :])
                for t in range(4):
                    free_after(c * 4, t, s_vl, pe)
                    pe.matmul(v_ps[:, t % 2, 0:GROUPS * D], ctxT[:, b, t * P:(t + 1) * P], wv[:, :],
                              start=True, stop=True).then_inc(s_v, 1)

            def pair(p, b, i):
                pe.wait_ge(s_wq[b], 16 * (i + 1))
                for k in range(4):
                    u = k % 2
                    project_item(p * 4 + 4 * CHUNKS, k, wq[:, b, k // 2, 0, :], wq[:, b, k // 2, 1, :],
                                 xT[:, u * UNIT:(u + 1) * UNIT])

            pe.wait_ge(s_const, 16 * 7)
            pe.wait_ge(s_x, 32)
            pe.wait_ge(s_ln, 9)
            for r in range(ROWS // P):
                pe.transpose(x_ps[:, r // 4, r % 4, :], xc[:, r, :], ident[:, :]).then_inc(s_xT, 1)
            through_chunks(pe, chunk)
            pe.wait_ge(s_xTs, 2)
            through_pairs(pe, pair)

        @block.vector
        def _(dve):
            def terms(n4, i, cos, sin):
                n = n4 + i + 1
                dve.wait_ge(s_proj, n)
                free_after(n4, i, s_rot, dve)
                dve.tensor_tensor(t_cos[:, i % 2, :], plain_ps[:, i % 2, :], cos, ALU.mult)
                dve.tensor_tensor(t_sin[:, i % 2, :], swap_ps[:, i % 2, :], sin, ALU.mult
                                  ).then_inc(s_terms, 1)

            def low(n4, i):
                dve.wait_ge(s_hi, n4 + i + 1)
                dve.tensor_tensor(parts[D:P, i, :], rot[D:P, i, :], parts[D:P, i, :].bitcast(F32),
                                  ALU.subtract).then_inc(s_lo, 1)

            def chunk(c, b, i):
                dve.wait_ge(s_masked, c + 1)
                for g in range(GROUPS):
                    terms(c * 4, g, cos_k[:, b, :], sin_k[:, b, :])
                    if g:
                        low(c * 4, g - 1)
                low(c * 4, GROUPS - 1)
                for t in range(4):
                    v = v_ps[:, t % 2, 0:GROUPS * D].rearrange("p (g n) -> p g n", g=GROUPS)
                    dve.wait_ge(s_vh, c * 4 + t + 1)
                    dve.tensor_tensor(vrest[:, t % 2], v, vst[:, b, :, t, 0:D], ALU.subtract
                                      ).then_inc(s_vr, 1)
                    dve.wait_ge(s_vm, c * 4 + t + 1)
                    dve.tensor_tensor(vst[:, b, :, t, VLO:VCOLS], vrest[:, t % 2], vst[:, b, :, t, D:2 * D],
                                      ALU.subtract).then_inc(s_vl, 1)

            def pair(p, b, i):
                for k in range(4):
                    u = k % 2
                    cols = slice(u * UNIT, (u + 1) * UNIT)
                    terms(p * 4 + 4 * CHUNKS, k, cos_q[:, cols], sin_q[:, cols])
                    if k:
                        low(p * 4 + 4 * CHUNKS, k - 1)
                low(p * 4 + 4 * CHUNKS, 3)

            dve.wait_ge(s_x, 32)
            layer_norm(dve, None, x[:, :, :], xc[:, :, :], sq[:, :, :], st, s_ln, s_sqrt, 0, 0,
                       float(D) ** -0.5, "dve")
            for half in range(2):
                dve.wait_ge(s_xT, 4 * (half + 1))
                dve.tensor_copy(xT[:, half * UNIT:(half + 1) * UNIT].rearrange("p (r n) -> p r n", r=4),
                                x_ps[:, half]).then_inc(s_xTs, 1)
            dve.wait_ge(s_const, 16 * 7)
            through_chunks(dve, chunk)
            through_pairs(dve, pair)

        @block.scalar
        def _(act):
            def high(n4, i):
                act.wait_ge(s_rot, n4 + i + 1)
                act.wait_ge(s_out, n4 * 16)
                act.activation(parts[:, i, :], rot[:, i, :], ACT.Copy).then_inc(s_hi, 1)

            def chunk(c, b, i):
                for g in range(GROUPS):
                    high(c * 4, g)
                act.wait_ge(s_vout, i * 32)
                for t in range(4):
                    v = v_ps[:, t % 2, 0:GROUPS * D].rearrange("p (g n) -> p g n", g=GROUPS)
                    act.wait_ge(s_v, c * 4 + t + 1)
                    act.activation(vst[:, b, :, t, 0:D], v, ACT.Copy).then_inc(s_vh, 1)
                    act.wait_ge(s_vr, c * 4 + t + 1)
                    act.activation(vst[:, b, :, t, D:2 * D], vrest[:, t % 2], ACT.Copy).then_inc(s_vm, 1)

            def pair(p, b, i):
                for k in range(4):
                    high(p * 4 + 4 * CHUNKS, k)

            layer_norm(None, act, x[:, :, :], xc[:, :, :], sq[:, :, :], st, s_ln, s_sqrt, 0, 0, 1.0, "act")
            through_chunks(act, chunk)
            through_pairs(act, pair)

        @block.gpsimd
        def _(pool):
            def rotate(n4, i):
                pool.wait_ge(s_terms, n4 + i + 1)
                pool.wait_ge(s_lo, n4)
                pool.tensor_tensor(rot[:, i, :], t_cos[:, i % 2, :], t_sin[:, i % 2, :], ALU.add
                                   ).then_inc(s_rot, 1)

            def chunk(c, b, i):
                pool.wait_ge(s_chunk[b], 96 * (i + 1))
                pool.tensor_tensor(cos_k[:, b, :], cos_k[:, b, :], maskf[:, b, :], ALU.mult)
                pool.tensor_tensor(sin_k[:, b, :], sin_k[:, b, :], maskf[:, b, :], ALU.mult
                                   ).then_inc(s_masked, 1)
                if c is CHUNKS - 1:
                    pool.wait_ge(s_vout, 16 * (CHUNKS - 2))
                    for g in range(GROUPS):
                        mm = pool.tensor_copy(vst[:, b, g, 4 - PAD_TILES:4, ONES], valid[:, :])
                    mm.then_inc(s_ones, 1)
                for g in range(GROUPS):
                    rotate(c * 4, g)

            def pair(p, b, i):
                for k in range(4):
                    rotate(p * 4 + 4 * CHUNKS, k)

            pool.dma_start(mask_scr, ins["mask_row"]).then_inc(s_maskf, 16)
            pool.memset(vst[:, :, :, :, ONES], 1.0).then_inc(s_ones, 1)
            pool.wait_ge(s_const, 16 * 7)
            through_chunks(pool, chunk)
            through_pairs(pool, pair)


def attend(nc, ins, k_scr, q_scr, v_scr, attn):
    with ExitStack() as ctx:
        def sb(name, shape, dt):
            return ctx.enter_context(nc.sbuf_tensor(name, shape, dt))

        def sem(name):
            return ctx.enter_context(nc.semaphore(name))

        kcols = TILES * P
        k_hilo = sb("k_hilo", [P, kcols], F32R)
        k_high = sb("k_high", [P, kcols], F32R)
        values = sb("values", [P, TILES, VCOLS], BF16)
        table = sb("table", [P, 2, TABLE], F32)
        q_hihi = sb("q_hihi", [P, HALVES, UNIT], F32R)
        q_low = sb("q_low", [P, HALVES, UNIT], F32R)
        q_seek = sb("q_seek", [P, HALVES, UNIT], F32R)
        prob = sb("prob", [P, S_BUFS, UNIT], F32)
        prob_lo = sb("prob_lo", [P, S_BUFS, UNIT], BF16)
        seen = sb("seen", [P, 2, PIECE], BF16)
        best = sb("best", [P, BLOCKS, PIECE], BF16)
        negmax = sb("negmax", [P, 4, BLOCKS], F32)
        negmax_r = sb("negmax_r", [P, 2, BLOCKS], F32R)
        diag = sb("diag", [P, 2, BLOCKS, P], F32R)
        pick = sb("pick", [P, 2, P], F32R)
        ident = sb("aident", [P, P], F32)
        row_const = sb("row_const", [P, 3], F32)
        pick_f = sb("pick_f", [P, 2, P], F32)
        mask_row = sb("mask_row", [P, kcols], U8)
        mask_col = sb("mask_col", [P, TILES], U8)
        keep = sb("keep", [P, TILES], F32)
        drop = sb("drop", [P, TILES], F32)
        last_bias = sb("last_bias", [P, HEADS], F32)
        far = sb("far", [P, HALVES, TILES], F32)
        far_one = sb("far_one", [P, HALVES], F32)
        o_sb = sb("o_sb", [P, HALVES, BLOCKS, VCOLS], F32)
        o_sum = sb("o_sum", [P, HALVES, BLOCKS, D], F32)
        rden = sb("rden", [P, HALVES, BLOCKS], F32)

        s_ps = ctx.enter_context(nc.psum_tensor("s_ps", [P, S_BUFS, 512], F32))
        a_ps = ctx.enter_context(nc.psum_tensor("a_ps", [P, 2, 512], F32))
        o_ps = ctx.enter_context(nc.psum_tensor("o_ps", [P, 2, 512], F32))

        s_c = sem("a_c")
        s_set = sem("a_set")
        s_k = [sem(f"a_k{c}") for c in range(PIECES)]
        s_val = [sem(f"a_val{c}") for c in range(PIECES)]
        s_qs = [sem("a_qs0"), sem("a_qs1")]
        s_q = [sem("a_q0"), sem("a_q1")]
        s_far = sem("a_far")
        s_tab = sem("a_tab")
        s_seek = sem("a_seek")
        s_add = sem("a_add")
        s_copy = sem("a_copy")
        s_best = sem("a_best")
        s_fold = sem("a_fold")
        s_diag = sem("a_diag")
        s_row = sem("a_row")
        s_max = sem("a_max")
        s_sc = sem("a_sc")
        s_band = sem("a_band")
        s_exp = sem("a_exp")
        s_lo = sem("a_lo")
        s_pv = sem("a_pv")
        s_o = sem("a_o")
        s_rden = sem("a_rden")
        s_osum = sem("a_osum")

        STEPS = HALVES * TILES
        FOLD_STEPS = 8
        prob_hi = prob[:, :, :].bitcast(BF16).rearrange("p s (n two) -> p s n two", two=2)

        def half_of(s):
            return s // TILES, s % TILES

        block = ctx.enter_context(nc.Block())

        @block.sync
        def _(sp):
            def load_keys(g, before):
                for c in range(PIECES):
                    lo, hi = c * PIECE_TILES, min((c + 1) * PIECE_TILES, TILES)
                    if before is not None:
                        sp.wait_ge(s_sc, before + hi)
                    cols = slice(lo * P, hi * P)
                    sp.dma_start(k_high[0:D, cols].bitcast(F32), k_scr[g, 0:D, cols]).then_inc(s_k[c], 16)
                    sp.dma_start(k_hilo[:, cols].bitcast(F32), k_scr[g, :, cols]).then_inc(s_k[c], 16)
                    if before is not None:
                        sp.wait_ge(s_pv, before + hi)
                    sp.dma_start(values[:, lo:hi, :],
                                 v_scr[g, :, lo * VCOLS:hi * VCOLS].rearrange("p (t n) -> p t n", n=VCOLS)
                                 ).then_inc(s_val[c], 16)

            def load_seek(h, u):
                sp.dma_start(q_seek[0:D, u, :].bitcast(F32), q_scr[h, 0:D, u * UNIT:(u + 1) * UNIT]
                             ).then_inc(s_qs[u], 16)

            def load_query(h, u):
                cols = slice(u * UNIT, (u + 1) * UNIT)
                sp.dma_start(q_hihi[0:D, u, :].bitcast(F32), q_scr[h, 0:D, cols]).then_inc(s_q[u], 16)
                sp.dma_start(q_hihi[D:P, u, :].bitcast(F32), q_scr[h, 0:D, cols]).then_inc(s_q[u], 16)
                sp.dma_start(q_low[0:D, u, :].bitcast(F32), q_scr[h, D:P, cols]).then_inc(s_q[u], 16)

            def load_table(h, b):
                sp.dma_start(table[:, b, :], ins["bias_rows"](h)).then_inc(s_tab, 16)

            def load_head(h, new_group):
                sp.wait_ge(s_seek, (h * 2 - 1) * SEEKS)
                load_seek(h, 0)
                sp.wait_ge(s_pv, (h - 1) * STEPS)
                load_table(h, h % 2)
                sp.wait_ge(s_sc, h * STEPS - TILES)
                load_query(h, 0)
                sp.wait_ge(s_seek, h * 2 * SEEKS)
                load_seek(h, 1)
                if new_group is not None:
                    load_keys(new_group, h * STEPS - TILES)
                sp.wait_ge(s_sc, h * STEPS)
                load_query(h, 1)

            sp.dma_start(mask_row[:, :],
                         ins["mask_row"][:, 0:kcols].to_broadcast([P, kcols])).then_inc(s_c, 16)
            sp.dma_start(mask_col[:, :], ins["mask_col"]).then_inc(s_c, 16)
            sp.dma_start(row_const[:, :], ins["row_const"]).then_inc(s_c, 16)
            sp.dma_start(pick_f[:, :, :], ins["pick"]).then_inc(s_c, 16)
            sp.dma_start(ident[:, :], ins["ident"]).then_inc(s_c, 16)
            sp.dma_start(last_bias[:, :], ins["last_bias"].to_broadcast([P, HEADS])).then_inc(s_c, 16)
            load_seek(0, 0)
            load_table(0, 0)
            load_keys(0, None)
            load_query(0, 0)
            load_seek(0, 1)
            load_query(0, 1)
            with sp.Fori(0, GROUPS - 1) as g:
                with sp.Fori(1, REP) as r:
                    load_head(g * REP + r, None)
                load_head(g * REP + REP, g + 1)
            with sp.Fori(HEADS - REP + 1, HEADS) as h:
                load_head(h, None)

        def through_heads(eng, search, head):
            with eng.Fori(0, GROUPS) as g:
                search(g * REP)
                with eng.Fori(0, REP - 1) as r:
                    head(g * REP + r, True)
                head(g * REP + (REP - 1), False)

        def searches(h, s, more):
            u, j = half_of(s)
            if u == 0:
                return h, 1, j
            return (h + 1, 0, j) if more else None

        def seek_free(eng, h, u, k):
            if k == 0:
                eng.wait_ge(s_max, h * 2 + u)
                return
            adds = sum(biased_piece(u, i % PIECES) for i in range(k))
            copies = k - adds
            if biased_piece(u, (k - 1) % PIECES):
                eng.wait_ge(s_add, h * sum(ADDS) + u * ADDS[0] + adds)
            else:
                eng.wait_ge(s_copy, h * sum(COPIES) + u * COPIES[0] + copies)

        @block.tensor
        def _(pe):
            def seek(h, u, j, first):
                for k in SEEK_AT.get(j, []):
                    r, c = divmod(k, PIECES)
                    if k == 0:
                        pe.wait_ge(s_qs[u], (h + 1) * 16)
                    if first is not None and r == 0:
                        pe.wait_ge(s_k[c], first * 32)
                    seek_free(pe, h, u, k)
                    width = piece_width(c)
                    for a in range(0, width, 512):
                        w = min(512, width - a)
                        mm = pe.matmul(a_ps[:, a // 512, 0:w], q_seek[:, u, r * P:(r + 1) * P],
                                       k_high[:, c * PIECE + a:c * PIECE + a + w], start=True, stop=True)
                    mm.then_inc(s_seek, 1)
                if j == ROWMAX_STEP:
                    pe.wait_ge(s_diag, h * 2 + u + 1)
                    seek_free(pe, h, u, SEEKS)
                    pe.matmul(a_ps[:, 0, :], pick[:, 0, :], diag[:, 0, :, :].rearrange("p b n -> p (b n)"),
                              start=True, stop=False)
                    pe.matmul(a_ps[:, 0, :], pick[:, 1, :], diag[:, 1, :, :].rearrange("p b n -> p (b n)"),
                              start=False, stop=True).then_inc(s_row, 1)

            def scores(h, s):
                u, t = half_of(s)
                if t == 0:
                    pe.wait_ge(s_q[u], (h + 1) * 48)
                    pe.wait_ge(s_max, h * 2 + u + 1)
                if s >= S_BUFS:
                    pe.wait_ge(s_exp, h * STEPS + s - S_BUFS + 1)
                cols = slice(t * P, (t + 1) * P)
                pe.matmul(s_ps[:, s % S_BUFS, :], k_hilo[:, cols], q_hihi[:, u, :], start=True, stop=False)
                pe.matmul(s_ps[:, s % S_BUFS, :], k_high[:, cols], q_low[:, u, :], start=False, stop=True
                          ).then_inc(s_sc, 1)

            def products(h, s, group_count):
                u, t = half_of(s)
                pe.wait_ge(s_lo, h * STEPS + s + 1)
                if t == 0:
                    pe.wait_ge(s_o, h * 2 + u)
                if u == 0 and t % PIECE_TILES == 0:
                    pe.wait_ge(s_val[t // PIECE_TILES], group_count * 16)
                for r in range(BLOCKS):
                    rows = slice(r * P, (r + 1) * P)
                    acc = o_ps[:, r // 2, (r % 2) * VCOLS:(r % 2 + 1) * VCOLS]
                    pe.matmul(acc, prob_hi[:, s % S_BUFS, rows, 1], values[:, t, :],
                              start=(t == 0 and r % 2 == 0), stop=False, skip_group_check=True)
                    mm = pe.matmul(acc[:, 0:VLO], prob_lo[:, s % S_BUFS, rows], values[:, t, 0:VLO],
                                   start=False, stop=(t == TILES - 1), skip_group_check=True)
                mm.then_inc(s_pv, 1)

            pe.wait_ge(s_set, 7)

            with pe.Fori(0, GROUPS) as g:
                for j in range(TILES):
                    seek(g * REP, 0, j, g + 1)

                def head(h, more):
                    for s in range(STEPS):
                        scores(h, s)
                        nxt = searches(h, s, more)
                        if nxt:
                            seek(*nxt, None)
                        if s >= LAG:
                            products(h, s - LAG, g + 1)
                    for s in range(STEPS - LAG, STEPS):
                        products(h, s, g + 1)

                with pe.Fori(0, REP - 1) as r:
                    head(g * REP + r, True)
                head(g * REP + (REP - 1), False)

        @block.scalar
        def _(act):
            def seek(h, u, j):
                if j == 0:
                    act.wait_ge(s_far, (h * 2 + u) * 2 + 1)
                for k in SEEK_AT.get(j, []):
                    r, c = divmod(k, PIECES)
                    if biased_piece(u, c):
                        continue
                    act.wait_ge(s_seek, (h * 2 + u) * SEEKS + k + 1)
                    m = r * (PIECES - 1) + c - 1
                    act.wait_ge(s_best, (h * 2 + u) * FOLDS + max(m - 1, 0))
                    w = piece_width(c)
                    act.activation(seen[:, m % 2, 0:w], a_ps[:, :, :].rearrange("p a n -> p (a n)")[:, 0:w],
                                   ACT.Identity, bias=far_one[:, u:u + 1]).then_inc(s_copy, 1)

            def exponentials(h, s):
                u, t = half_of(s)
                if t == 0:
                    act.wait_ge(s_far, (h * 2 + u) * 2 + 2)
                if t in BAND[u]:
                    done = len(BAND[0]) * u + BAND[u].index(t) + 1
                    act.wait_ge(s_band, h * BAND_PER_HEAD + done)
                    bias = drop[:, t:t + 1]
                else:
                    act.wait_ge(s_sc, h * STEPS + s + 1)
                    bias = far[:, u, t:t + 1]
                if s >= S_BUFS:
                    act.wait_ge(s_pv, h * STEPS + s - S_BUFS + 1)
                act.activation(prob[:, s % S_BUFS, :], s_ps[:, s % S_BUFS, :], ACT.Exp, bias=bias
                               ).then_inc(s_exp, 1)

            def take_sums(h, u):
                act.wait_ge(s_pv, h * STEPS + (u + 1) * TILES)
                act.wait_ge(s_osum, (h * 2) * 3)
                act.activation(o_sb[:, u, :, :].rearrange("p (a b) n -> p a (b n)", b=2),
                               o_ps[:, :, 0:2 * VCOLS], ACT.Copy).then_inc(s_o, 1)

            def search(h):
                for j in range(TILES):
                    seek(h, 0, j)

            def head(h, more):
                for s in range(STEPS):
                    exponentials(h, s)
                    if s == TILES + LAG:
                        take_sums(h, 0)
                    nxt = searches(h, s, more)
                    if nxt:
                        seek(*nxt)
                take_sums(h, 1)

            act.wait_ge(s_set, 7)
            through_heads(act, search, head)

        @block.vector
        def _(dve):
            def add_near(h, u, k):
                r, c = divmod(k, PIECES)
                dve.wait_ge(s_seek, (h * 2 + u) * SEEKS + k + 1)
                m = r * (PIECES - 1) + c - 1
                w = piece_width(c)
                if c == 0:
                    to = best[:, r, :]
                    if k == 0:
                        dve.wait_ge(s_tab, (h + 1) * 16)
                        dve.wait_ge(s_fold, (h * 2 + u) * FOLD_STEPS)
                else:
                    to = seen[:, m % 2, :]
                    dve.wait_ge(s_best, (h * 2 + u) * FOLDS + max(m - 1, 0))
                first = c * PIECE + u * UNIT + r * P
                dve.tensor_tensor(to, a_ps[:, :, :].rearrange("p a n -> p (a n)"),
                                  table[:, bass.ds(h % 2, 1), first:first + w].rearrange("p o n -> p (o n)"),
                                  ALU.add).then_inc(s_add, 1)

            def take_best(h, u, k):
                r, c = divmod(k, PIECES)
                if c == 0:
                    return
                m = r * (PIECES - 1) + c - 1
                upto = [biased_piece(u, i % PIECES) for i in range(k + 1)]
                if upto[k]:
                    dve.wait_ge(s_add, h * sum(ADDS) + u * ADDS[0] + sum(upto))
                else:
                    dve.wait_ge(s_copy, h * sum(COPIES) + u * COPIES[0] + k + 1 - sum(upto))
                if c == 1:
                    dve.wait_ge(s_add, h * sum(ADDS) + u * ADDS[0]
                                + sum(biased_piece(u, i % PIECES) for i in range(k)))
                dve.wait_ge(s_best, (h * 2 + u) * FOLDS + m)
                w = piece_width(c)
                dve.tensor_tensor(best[:, r, 0:w], best[:, r, 0:w], seen[:, m % 2, 0:w], ALU.max
                                  ).then_inc(s_best, 1)

            def after_search(h, u, j):
                n = (h * 2 + u) * FOLD_STEPS
                if FOLD_STEP <= j < FOLD_STEP + 4:
                    i = j - FOLD_STEP
                    w = PIECE >> (i + 1)
                    if i == 0:
                        dve.wait_ge(s_best, (h * 2 + u + 1) * FOLDS)
                        dve.wait_ge(s_fold, n)
                    else:
                        dve.wait_ge(s_fold, n + i)
                    dve.tensor_tensor(best[:, :, 0:w], best[:, :, 0:w], best[:, :, w:2 * w], ALU.max
                                      ).then_inc(s_fold, 1)
                if j == SPLIT_STEP:
                    dve.wait_ge(s_fold, n + 4)
                    dve.tensor_reduce(negmax[:, 0, :], best[:, :, 0:64], AX.X, ALU.max).then_inc(s_fold, 1)
                    dve.wait_ge(s_fold, n + 5)
                    dve.tensor_scalar(negmax[:, 1, :], negmax[:, 0, :], -1.0, -MASKED, ALU.mult, ALU.min
                                      ).then_inc(s_fold, 1)
                    dve.wait_ge(s_fold, n + 6)
                    dve.tensor_copy(negmax_r[:, 0, :], negmax[:, 1, :]).then_inc(s_fold, 1)
                    dve.wait_ge(s_fold, n + 7)
                    dve.tensor_tensor(negmax_r[:, 1, :], negmax[:, 1, :], negmax_r[:, 0, :].bitcast(F32),
                                      ALU.subtract).then_inc(s_fold, 1)
                if j == SPLIT_STEP + 1:
                    dve.wait_ge(s_fold, n + 8)
                    dve.wait_ge(s_row, h * 2 + u)
                    for i in range(2):
                        mm = dve.tensor_tensor(
                            diag[:, i, :, :], ident[:, :].unsqueeze(1).to_broadcast([P, BLOCKS, P]),
                            negmax_r[:, i, :].bitcast(F32).unsqueeze(2).to_broadcast([P, BLOCKS, P]), ALU.mult)
                    mm.then_inc(s_diag, 1)
                if j == ROWMAX_STEP + 1:
                    dve.wait_ge(s_row, h * 2 + u + 1)
                    dve.tensor_copy(q_low[D:P, u, :], a_ps[D:P, 0, :]).then_inc(s_max, 1)

            def set_far(h, u):
                n = (h * 2 + u) * 2
                dve.wait_ge(s_far, n)
                dve.tensor_copy(far_one[:, u:u + 1], last_bias[:, bass.ds(h, 1)]).then_inc(s_far, 1)
                dve.wait_ge(s_far, n + 1)
                dve.scalar_tensor_tensor(out=far[:, u, :], in0=keep[:, :], scalar=far_one[:, u:u + 1],
                                         in1=drop[:, :], op0=ALU.mult, op1=ALU.add).then_inc(s_far, 1)

            def seek(h, u, j):
                if j == 0:
                    set_far(h, u)
                for k in SEEK_AT.get(j - 1, []):
                    take_best(h, u, k)
                for k in SEEK_AT.get(j, []):
                    if biased_piece(u, k % PIECES):
                        add_near(h, u, k)
                after_search(h, u, j)

            def near_bias(h, s):
                u, t = half_of(s)
                if t in BAND[u]:
                    dve.wait_ge(s_sc, h * STEPS + s + 1)
                    first = t * P + u * UNIT
                    dve.scalar_tensor_tensor(
                        out=s_ps[:, s % S_BUFS, :],
                        in0=table[:, bass.ds(h % 2, 1), first:first + UNIT].rearrange("p o n -> p (o n)"),
                        scalar=keep[:, t:t + 1], in1=s_ps[:, s % S_BUFS, :], op0=ALU.mult, op1=ALU.add
                    ).then_inc(s_band, 1)

            def low_part(h, s):
                dve.wait_ge(s_exp, h * STEPS + s + 1)
                dve.tensor_tensor(prob_lo[:, s % S_BUFS, :], prob[:, s % S_BUFS, :],
                                  prob_hi[:, s % S_BUFS, :, 1], ALU.subtract).then_inc(s_lo, 1)

            def invert(h, u):
                dve.wait_ge(s_o, h * 2 + u + 1)
                dve.wait_ge(s_osum, h * 6)
                dve.reciprocal(rden[:, u, :], o_sb[:, u, :, ONES]).then_inc(s_rden, 1)

            def search(h):
                for j in range(TILES):
                    seek(h, 0, j)

            def head(h, more):
                for s in range(STEPS):
                    near_bias(h, s)
                    if s:
                        low_part(h, s - 1)
                    if s == TILES + LAG + 2:
                        invert(h, 0)
                    nxt = searches(h, s, more)
                    if nxt:
                        seek(*nxt)
                low_part(h, STEPS - 1)
                invert(h, 1)

            dve.wait_ge(s_c, 16 * 6)
            dve.tensor_scalar(k_high[D:P, :], mask_row[D:P, :], row_const[D:P, 0:1], row_const[D:P, 1:2],
                              ALU.mult, ALU.add).then_inc(s_set, 1)
            dve.memset(prob[:, :, :], 0.0).then_inc(s_set, 1)
            dve.wait_ge(s_set, 2)
            for u in range(HALVES):
                dve.tensor_scalar(q_seek[D:P, u, :], prob[D:P, u, :], row_const[D:P, 2:3], None,
                                  ALU.add).then_inc(s_set, 1)
            dve.tensor_copy(pick[:, :, :], pick_f[:, :, :]).then_inc(s_set, 1)
            dve.tensor_copy(keep[:, :], mask_col[:, :]).then_inc(s_set, 1)
            dve.wait_ge(s_set, 6)
            dve.tensor_scalar(drop[:, :], keep[:, :], -MASKED, MASKED, ALU.mult, ALU.add).then_inc(s_set, 1)
            dve.wait_ge(s_set, 7)
            through_heads(dve, search, head)

        @block.gpsimd
        def _(pool):
            with pool.Fori(0, HEADS) as h:
                for u in range(HALVES):
                    n = h * 6 + u * 3
                    pool.wait_ge(s_o, h * 2 + u + 1)
                    pool.tensor_tensor(o_sum[:, u], o_sb[:, u, :, 0:D], o_sb[:, u, :, D:2 * D], ALU.add
                                       ).then_inc(s_osum, 1)
                    pool.wait_ge(s_osum, n + 1)
                    pool.tensor_tensor(o_sum[:, u], o_sum[:, u], o_sb[:, u, :, VLO:VCOLS], ALU.add
                                       ).then_inc(s_osum, 1)
                    pool.wait_ge(s_osum, n + 2)
                    pool.wait_ge(s_rden, h * 2 + u + 1)
                    pool.tensor_tensor(attn[:, u * BLOCKS:(u + 1) * BLOCKS, bass.ds(h * D, D)], o_sum[:, u],
                                       rden[:, u, :].unsqueeze(2).to_broadcast([P, BLOCKS, D]), ALU.mult
                                       ).then_inc(s_osum, 1)


def finish(nc, ins, attn, out):
    with ExitStack() as ctx:
        def sb(name, shape, dt):
            return ctx.enter_context(nc.sbuf_tensor(name, shape, dt))

        def sem(name):
            return ctx.enter_context(nc.semaphore(name))

        NB = ROWS // P
        NE = HEADS * D // P
        x = sb("fx", [P, NB, DM], F32)
        x1 = sb("x1", [P, NB, DM], F32)
        xc = sb("fxc", [P, NB, DM], F32)
        sq = sb("fsq", [P, NB, DM], F32)
        st = sb("fst", [P, 4, NB], F32)
        res = sb("res", [P, NB, DM], F32)
        ident = sb("fident", [P, P], F32)
        wo = sb("wo", [P, NE, DM], F32)
        w = sb("w", [DM, 3, DM], F32)
        bias = sb("bias", [DM, 1], F32)
        attnT = sb("attnT", [P, 2, ROWS], F32)
        hT = sb("hT", [DM, 5, ROWS], F32)

        tr = ctx.enter_context(nc.psum_tensor("tr", [P, 4, 512], F32))
        acc = ctx.enter_context(nc.psum_tensor("acc", [P, 2, 512], F32))

        s_in = sem("f_in")
        s_tr = sem("f_tr")
        s_ev = sem("f_ev")
        s_ev2 = sem("f_ev2")
        s_acc = sem("f_acc")
        s_t = sem("f_t")
        s_y = sem("f_y")
        s_mm = sem("f_mm")
        s_ln = sem("f_ln")
        s_sqrt = sem("f_sqrt")
        s_x1 = sem("f_x1")
        s_res = sem("f_res")
        s_out = sem("f_out")

        block = ctx.enter_context(nc.Block())

        def tr_bank(i):
            return tr[:, i % 4, :]

        @block.sync
        def _(sp):
            sp.dma_start(ident[:, :], ins["ident"]).then_inc(s_in, 16)
            sp.dma_start(wo[:, :, :], ins["wo"]).then_inc(s_in, 16)
            sp.dma_start(x[:, :, :], ins["x"]).then_inc(s_in, 16)
            sp.dma_start(w[:, :, :], ins["w"]).then_inc(s_in, 16)
            sp.dma_start(bias[:, :], ins["bias"]).then_inc(s_in, 16)
            for half in range(2):
                sp.wait_ge(s_res, half + 1)
                sp.dma_start(out[:, half * 4:(half + 1) * 4, :], res[:, half * 4:(half + 1) * 4, :]
                             ).then_inc(s_out, 16)
            sp.wait_ge(s_out, 32)

        @block.tensor
        def _(pe):
            pe.wait_ge(s_in, 80)
            for e in range(NE + 1):
                if e < NE:
                    for half in range(2):
                        if e >= 2:
                            pe.wait_ge(s_ev if half == 0 else s_ev2, e - 1)
                        for q in range(4):
                            mm = pe.transpose(tr[:, (2 * e + half) % 4, q * P:(q + 1) * P],
                                              attn[:, half * 4 + q, e * P:(e + 1) * P], ident[:, :])
                        mm.then_inc(s_tr, 1)
                if e >= 1:
                    pe.wait_ge(s_ev, e)
                    pe.wait_ge(s_ev2, e)
                    for half in range(2):
                        mm = pe.matmul(acc[:, half, :], wo[:, e - 1, :],
                                       attnT[:, (e - 1) % 2, half * 512:(half + 1) * 512],
                                       start=(e == 1), stop=(e == NE))
                    mm.then_inc(s_acc, 1)
            for half in range(2):
                pe.wait_ge(s_t, half + 1)
                for q in range(4):
                    mm = pe.transpose(tr[:, half, q * P:(q + 1) * P],
                                      hT[:, 0, (half * 4 + q) * P:(half * 4 + q + 1) * P], ident[:, :])
                mm.then_inc(s_tr, 1)
            pe.wait_ge(s_ln, 9)
            for half in range(2):
                for q in range(4):
                    mm = pe.transpose(tr[:, 2 + half, q * P:(q + 1) * P], xc[:, half * 4 + q, :], ident[:, :])
                mm.then_inc(s_tr, 1)
            for i in range(3):
                for half in range(2):
                    pe.wait_ge(s_t, 2 + 2 * i + half + 1)
                    pe.matmul(acc[:, half, :], w[:, i, :], hT[:, 1 + i, half * 512:(half + 1) * 512],
                              start=True, stop=True).then_inc(s_mm, 1)
            for half in range(2):
                pe.wait_ge(s_y, half + 1)
                for q in range(4):
                    mm = pe.transpose(tr[:, half, q * P:(q + 1) * P],
                                      hT[:, 4, (half * 4 + q) * P:(half * 4 + q + 1) * P], ident[:, :])
                mm.then_inc(s_tr, 1)

        @block.vector
        def _(dve):
            dve.wait_ge(s_in, 80)
            for e in range(NE):
                dve.wait_ge(s_tr, 2 * e + 1)
                if e >= 2:
                    dve.wait_ge(s_acc, e - 1)
                dve.tensor_copy(attnT[:, e % 2, 0:512], tr[:, (2 * e) % 4, :]).then_inc(s_ev, 1)
            for half in range(2):
                dve.wait_ge(s_acc, NE)
                dve.tensor_copy(hT[:, 0, half * 512:(half + 1) * 512], acc[:, half, :]).then_inc(s_t, 1)
            for half in range(2):
                dve.wait_ge(s_tr, 2 * NE + half + 1)
                rows = slice(half * 4, half * 4 + 4)
                dve.tensor_tensor(x1[:, rows, :], tr[:, half, :].rearrange("p (q n) -> p q n", q=4), x[:, rows, :],
                                  ALU.add).then_inc(s_x1, 1)
            dve.wait_ge(s_x1, 2)
            layer_norm(dve, None, x1[:, :, :], xc[:, :, :], sq[:, :, :], st, s_ln, s_sqrt, 0, 0, 1.0, "dve")
            for half in range(2):
                dve.wait_ge(s_tr, 2 * NE + 2 + half + 1)
                dve.tensor_copy(hT[:, 1, half * 512:(half + 1) * 512], tr[:, 2 + half, :]).then_inc(s_t, 1)
            for i in range(2):
                for half in range(2):
                    dve.wait_ge(s_mm, 2 * i + half + 1)
                    dve.tensor_copy(hT[:, 2 + i, half * 512:(half + 1) * 512], acc[:, half, :]).then_inc(s_t, 1)
            for half in range(2):
                dve.wait_ge(s_tr, 2 * NE + 4 + half + 1)
                rows = slice(half * 4, half * 4 + 4)
                dve.tensor_tensor(res[:, rows, :], tr[:, half, :].rearrange("p (q n) -> p q n", q=4),
                                  x1[:, rows, :], ALU.add).then_inc(s_res, 1)

        @block.scalar
        def _(act):
            for e in range(NE):
                act.wait_ge(s_tr, 2 * e + 2)
                if e >= 2:
                    act.wait_ge(s_acc, e - 1)
                act.copy(attnT[:, e % 2, 512:1024], tr[:, (2 * e + 1) % 4, :]).then_inc(s_ev2, 1)
            layer_norm(None, act, x1[:, :, :], xc[:, :, :], sq[:, :, :], st, s_ln, s_sqrt, 0, 0, 1.0, "act")
            for half in range(2):
                act.wait_ge(s_mm, 4 + half + 1)
                act.activation(hT[:, 4, half * 512:(half + 1) * 512], acc[:, half, :], ACT.Tanh,
                               bias=bias[:, 0:1]).then_inc(s_y, 1)


def build(nc, aps):
    ins = dict(aps)
    ext = aps["bias_ext"]

    def bias_rows(h):
        row = ext[bass.ds(h, 1), 0:TABLE]
        return overlapped(row)

    def overlapped(row):
        return bass.AP(row.tensor, row.offset, [[1, P], [1, TABLE]])

    ins["bias_rows"] = bias_rows
    attention(nc, ins, aps["out"])


def kernel(x, ctx_1024, mask_BxS2_bf1, L0_xattn_Wq, L0_xattn_Wk, L0_xattn_Wv, L0_xattn_Wo,
           L0_xattn_rel_pos_bias, L0_ffn_weight, L0_ffn_aux_weight1, L0_ffn_aux_weight2, L0_ffn_bias):
    import numpy as np
    import concourse.bacc as bacc
    from concourse.bass_utils import run_bass_kernel_spmd

    f32 = np.float32

    xr = np.asarray(x)[0, ::-1].reshape(ROWS // P, P, DM).transpose(1, 0, 2)
    ctxT = np.zeros((DM, KEYS_PAD), f32)
    ctxT[:, :KEYS] = np.asarray(ctx_1024)[0].T
    mask = np.zeros((KEYS_PAD,), bool)
    mask[:KEYS] = np.asarray(mask_BxS2_bf1)[0]
    mask_col = mask.reshape(-1, P).T[:, :TILES]

    expo = (np.arange(0, D, 2, dtype=f32) / f32(D)).astype(np.float64)
    inv = (f32(1) / (10000.0 ** expo).astype(f32)).astype(f32)
    inv = np.repeat(inv, 2)[:, None]
    sign = np.where(np.arange(D) < D // 2, -1.0, 1.0).astype(f32)[:, None]
    angle_k = (inv * np.arange(KEYS_PAD, dtype=f32)[None, :]).astype(np.float64)
    angle_q = (inv * np.arange(ROWS, dtype=f32)[None, ::-1]).astype(np.float64)

    def heads_twice(w, n):
        w = np.asarray(w).reshape(DM, n, D)
        swapped = np.concatenate([w[:, :, D // 2:], w[:, :, :D // 2]], axis=2)
        return np.stack([np.concatenate([w, w], 2), np.concatenate([swapped, swapped], 2)], axis=2)

    ext = np.abs(np.arange(TABLE + P) - (ROWS - 1)).clip(0, CLIP)
    bias_ext = np.asarray(L0_xattn_rel_pos_bias)[:, ext]
    row_const = np.zeros((P, 3), f32)
    row_const[ROW_PEN, 0], row_const[ROW_PEN, 1] = PEN, -PEN
    row_const[[ROW_NEGMAX_HI, ROW_NEGMAX_LO], 1] = 1.0
    row_const[ROW_PEN, 2] = 1.0
    pick = np.zeros((P, 2, P), f32)
    pick[:, 0, ROW_NEGMAX_HI] = 1.0
    pick[:, 1, ROW_NEGMAX_LO] = 1.0

    arrays = {
        "x": xr, "ctxT": ctxT, "mask_row": mask[None, :], "mask_col": mask_col,
        "wq": heads_twice(L0_xattn_Wq, HEADS), "wk": heads_twice(L0_xattn_Wk, GROUPS),
        "wv": np.asarray(L0_xattn_Wv),
        "wo": np.asarray(L0_xattn_Wo).reshape(-1, P, DM).transpose(1, 0, 2),
        "w": np.stack([np.asarray(a) for a in (L0_ffn_weight, L0_ffn_aux_weight1, L0_ffn_aux_weight2)], axis=1),
        "bias": np.asarray(L0_ffn_bias)[:, None],
        "bias_ext": bias_ext, "last_bias": np.asarray(L0_xattn_rel_pos_bias)[:, CLIP][None, :],
        "cos_k": np.cos(angle_k).astype(f32), "sin_k": (sign * np.sin(angle_k)).astype(f32),
        "cos_q": np.cos(angle_q).astype(f32), "sin_q": (sign * np.sin(angle_q)).astype(f32),
        "valid": (np.arange(KEYS_PAD).reshape(-1, P).T[:, -PAD_TILES:] < KEYS).astype(f32),
        "ident": np.eye(P, dtype=f32), "row_const": row_const, "pick": pick,
    }
    arrays = {"in_" + k: np.ascontiguousarray(v) for k, v in arrays.items()}
    nc = bacc.Bacc("TRN2", target_bir_lowering=False, num_devices=1)
    aps = {k[3:]: nc.dram_tensor(k, v.shape, mybir.dt.from_np(v.dtype), kind="ExternalInput").ap()
           for k, v in arrays.items()}
    aps["out"] = nc.dram_tensor("out", (P, ROWS // P, DM), F32, kind="ExternalOutput").ap()
    build(nc, aps)
    got = run_bass_kernel_spmd(nc, [arrays], core_ids=[0]).results[0]["out"]
    return np.ascontiguousarray(got.transpose(1, 0, 2).reshape(ROWS, DM)[::-1])[None]
```

```python
from contextlib import ExitStack

import concourse.bass as bass
from concourse import mybir

ALU = mybir.AluOpType
ACT = mybir.ActivationFunctionType
AX = mybir.AxisListType
F32 = mybir.dt.float32
F32R = mybir.dt.float32r
BF16 = mybir.dt.bfloat16
F16 = mybir.dt.float16
I32 = mybir.dt.int32
U8 = mybir.dt.uint8

P = 128
ROWS = 1024
KEYS = 6404
DM = 128
HEADS = 16
GROUPS = 4
REP = HEADS // GROUPS
D = 64
CLIP = 383
ALL_TILES = -(-KEYS // 256) * 2
KEYS_PAD = ALL_TILES * P
PAD_TILES = ALL_TILES - KEYS // P
TILES = -(-KEYS // P)
KEY_ITEMS = ALL_TILES // 2
QUERY_ITEMS = ROWS // P * 2
RING = 4
FIRST_TILES = 12
TABLE_TILES = (slice(0, FIRST_TILES), slice(FIRST_TILES, ALL_TILES))
UNIT = 512
HALVES = ROWS // UNIT
BLOCKS = UNIT // P
VCOLS = 2 * D + 1
ONES = 2 * D
MASKED = -1.0e9
PEN = float(2 ** 30)
ROW_NEGMAX_HI, ROW_PEN, ROW_NEGMAX_LO = 64, 65, 96
EPS = 1e-5

PIECE = 512
PIECES = -(-KEYS // PIECE)
SEEKS = BLOCKS * PIECES
LOAD = 2 * PIECE
LOADS = -(-KEYS // LOAD)
LOAD_TILES = LOAD // P
A_BUFS = 3
S_BUFS = 3
P_BUFS = 6
STEPS = HALVES * TILES
assert STEPS % S_BUFS == 0 and STEPS % P_BUFS == 0
LAG = 3
TURN = 6


def piece_width(c):
    return min(PIECE, KEYS - c * PIECE)


def any_near(low, keys, rows):
    return low + keys - 1 + rows - 1 > ROWS - 1 - CLIP and low < ROWS - 1 + CLIP


def near_piece(half, k):
    r, c = divmod(k, PIECES)
    return any_near(c * PIECE + half * UNIT + r * P, piece_width(c), P)


BAND = [[t for t in range(TILES) if any_near(t * P + u * UNIT, P, UNIT)] for u in range(HALVES)]
BAND_PER_HEAD = sum(map(len, BAND))
NEAR = [[k for k in range(SEEKS) if near_piece(u, k)] for u in range(HALVES)]
COPIES = [SEEKS - len(near) for near in NEAR]
JOINS = BLOCKS * (PIECES - 1)
TABLE = max([t * P + u * UNIT + UNIT for u in range(HALVES) for t in BAND[u]]
            + [k % PIECES * PIECE + k // PIECES * P + u * UNIT + PIECE for u in range(HALVES) for k in NEAR[u]])

LAST_SEEK = 41
SEEK_AT = {}
for _k in range(SEEKS):
    SEEK_AT.setdefault(_k * LAST_SEEK // SEEKS, []).append(_k)
FOLD_STEP = LAST_SEEK + 1
ROW_STEP = FOLD_STEP + 3
FOLDS = 3
AFTER_STEPS = FOLDS + 4

POOL_TILES = [t for t in range(13, TILES) if t % 5 == 3]


def attention(nc, ins, out):
    outer = ExitStack()
    with outer:
        scr = {"k": nc.dram_tensor("k_scr", [2, GROUPS * D, KEYS_PAD], F32, kind="Internal").ap(),
               "q": nc.dram_tensor("q_scr", [2, HEADS * D, ROWS], F32, kind="Internal").ap(),
               "v": nc.dram_tensor("v_scr", [GROUPS, P, ALL_TILES * VCOLS], F16, kind="Internal").ap()}
        v_scale = outer.enter_context(nc.sbuf_tensor("v_scale", [P, 1], F32))
        project(nc, ins, scr, v_scale)
        attn = outer.enter_context(nc.sbuf_tensor("attn", [P, ROWS // P, HEADS * D], F32))
        den = outer.enter_context(nc.sbuf_tensor("den", [P, ROWS // P, HEADS], F32))
        attend(nc, ins, scr, v_scale, attn, den)
        finish(nc, ins, attn, den, out)


def layer_norm(dve, act, x, xc, sq, st, s_dve, s_act, base_dve, base_act, factor, role):
    mean, var, sd, rs = (st[:, i, :] for i in range(4))
    wide = x.shape
    if role == "act":
        act.wait_ge(s_dve, base_dve + 6)
        act.activation(sd, var, ACT.Sqrt).then_inc(s_act, 1)
        return
    dve.tensor_reduce(mean, x, AX.X, ALU.add).then_inc(s_dve, 1)
    dve.wait_ge(s_dve, base_dve + 1)
    dve.tensor_scalar(mean, mean, -1.0 / DM, None, ALU.mult).then_inc(s_dve, 1)
    dve.wait_ge(s_dve, base_dve + 2)
    dve.tensor_tensor(xc, x, mean.unsqueeze(2).to_broadcast(wide), ALU.add).then_inc(s_dve, 1)
    dve.wait_ge(s_dve, base_dve + 3)
    dve.tensor_tensor(sq, xc, xc, ALU.mult).then_inc(s_dve, 1)
    dve.wait_ge(s_dve, base_dve + 4)
    dve.tensor_reduce(var, sq, AX.X, ALU.add).then_inc(s_dve, 1)
    dve.wait_ge(s_dve, base_dve + 5)
    dve.tensor_scalar(var, var, 1.0 / DM, EPS, ALU.mult, ALU.add).then_inc(s_dve, 1)
    dve.wait_ge(s_act, base_act + 1)
    dve.reciprocal(rs, sd).then_inc(s_dve, 1)
    dve.wait_ge(s_dve, base_dve + 7)
    dve.tensor_scalar(rs, rs, factor, None, ALU.mult).then_inc(s_dve, 1)
    dve.wait_ge(s_dve, base_dve + 8)
    dve.tensor_tensor(xc, xc, rs.unsqueeze(2).to_broadcast(wide), ALU.mult).then_inc(s_dve, 1)


def project(nc, ins, scr, v_scale):
    with ExitStack() as ctx:
        def sb(name, shape, dt):
            return ctx.enter_context(nc.sbuf_tensor(name, shape, dt))

        def sem(name):
            return ctx.enter_context(nc.semaphore(name))

        x = sb("x", [P, ROWS // P, DM], F32)
        xc = sb("xc", [P, ROWS // P, DM], F32)
        sq = sb("sq", [P, ROWS // P, DM], F32)
        st = sb("st", [P, 4, ROWS // P], F32)
        xT = sb("xT", [DM, ROWS], F32)
        ident = sb("ident", [P, P], F32)
        wk = sb("wk", [DM, GROUPS * D], F32)
        wv = sb("wv", [DM, GROUPS * D], F32)
        wq = sb("wq", [DM, HEADS * D], F32)
        cos_q = sb("cos_q", [P, ROWS // P, D], F32)
        sin_q = sb("sin_q", [P, ROWS // P, D], F32)
        cos_k = sb("cos_k", [P, ALL_TILES, D], F32)
        sin_k = sb("sin_k", [P, ALL_TILES, D], F32)
        mask_in = sb("mask_in", [P, ALL_TILES], U8)
        maskf = sb("maskf", [P, ALL_TILES], F32)
        valid = sb("valid", [P, PAD_TILES], F32)
        ctxT = sb("ctxT", [DM, RING, 2 * P], F32)
        fresh = sb("fresh", [DM, RING], F32)
        largest = sb("largest", [DM, RING], F32)
        bound = sb("bound", [P, 8], F32)
        ones = sb("ones", [P, P], F32)
        t_cos = sb("t_cos", [P, 2, 512], F32)
        t_sin = sb("t_sin", [P, 2, 512], F32)
        rot = sb("rot", [P, 2, 512], F32)
        parts = sb("parts", [P, RING, 2, 512], F32R)
        vst = sb("vst", [P, RING, GROUPS, 2, VCOLS], F16)

        prod = ctx.enter_context(nc.psum_tensor("prod", [P, 2, 512], F32))
        turned = ctx.enter_context(nc.psum_tensor("turned", [P, 2, 512], F32))
        v_ps = ctx.enter_context(nc.psum_tensor("v_ps", [P, 2, 512], F32))
        x_ps = ctx.enter_context(nc.psum_tensor("x_ps", [P, 2, 4, P], F32))

        s_x = sem("p_x")
        s_mask = sem("p_mask")
        s_w = sem("p_w")
        s_tab = [sem("p_tab0"), sem("p_tab1")]
        s_late = sem("p_late")
        s_ctx = [sem(f"p_ctx{i}") for i in range(RING)]
        s_ln = sem("p_ln")
        s_sqrt = sem("p_sqrt")
        s_xT = sem("p_xT")
        s_xTs = sem("p_xTs")
        s_maskf = sem("p_maskf")
        s_masked = sem("p_masked")
        s_big = sem("p_big")
        s_run = sem("p_run")
        s_bnd = sem("p_bnd")
        s_bmm = sem("p_bmm")
        s_proj = sem("p_proj")
        s_terms = sem("p_terms")
        s_rot = sem("p_rot")
        s_turn = sem("p_turn")
        s_hi = sem("p_hi")
        s_lo = sem("p_lo")
        s_out = [sem(f"p_out{i}") for i in range(RING)]
        s_v = sem("p_v")
        s_vh = sem("p_vh")
        s_vl = sem("p_vl")
        s_ones = sem("p_ones")
        s_vout = [sem(f"p_vout{i}") for i in range(RING)]

        k_dst = scr["k"].rearrange("part (pair p) k -> part p pair k", p=P)
        q_dst = scr["q"].rearrange("part (pair p) k -> part p pair k", p=P)

        def after(eng, sem_, value):
            if not isinstance(value, int) or value > 0:
                eng.wait_ge(sem_, value)

        def through(eng, first, count, early, ahead=0, late=None):
            def step(n, place, turn, with_early=True, with_late=True):
                if with_early:
                    early(n, place, turn)
                if late is not None and with_late:
                    back = place - ahead
                    late(n - ahead, back % RING, turn if back >= 0 else turn - 1)

            start = first + RING + ahead
            loops = (first + count - start) // RING if count > QUERY_ITEMS else 0
            for n in range(first, start):
                step(n, n % RING, n // RING, with_late=n - ahead >= first)
            if loops:
                with eng.Fori(0, loops) as j:
                    for i in range(start, start + RING):
                        step(j * RING + i, i % RING, j + i // RING)
            for n in range(start + loops * RING, first + count + ahead):
                step(n, n % RING, n // RING, with_early=n < first + count)

        block = ctx.enter_context(nc.Block())

        @block.sync
        def _(sp):
            def load_context(n, place, v=None):
                tile = n if v is None else v
                sp.dma_start(ctxT[:, place, :], ins["ctxT"][:, bass.ds(tile * 2 * P, 2 * P)]
                             ).then_inc(s_ctx[place], 16)

            def store(n, place, dst):
                sp.wait_ge(s_lo, n + 1)
                for part in range(2):
                    sp.dma_start(dst(part), parts[:, place, part, :].bitcast(F32).rearrange(
                        "p (a n) -> p a n", n=dst(part).shape[2])).then_inc(s_out[place], 16)

            def keys(n, place, turn):
                sp.wait_ge(s_proj, n + 1)
                sp.wait_ge(s_big, n + 1)
                if isinstance(n, int) and n + RING >= KEY_ITEMS:
                    load_context(n, place=(n + RING) % RING, v=n + RING - KEY_ITEMS)
                else:
                    load_context(n + RING, place)
                store(n, place, lambda part: k_dst[part, :, :, bass.ds(n * 2 * P, 2 * P)])

            def queries(n, place, turn):
                r, half = divmod(n - KEY_ITEMS, 2)
                store(n, place, lambda part: q_dst[part, :, half * 4:(half + 1) * 4, r * P:(r + 1) * P])

            def values(n, place, turn):
                v = n - KEY_ITEMS
                if not isinstance(n, int) or v + RING < KEY_ITEMS:
                    sp.wait_ge(s_v, v + 1)
                    load_context(n, place, v + RING)
                sp.wait_ge(s_vl, v + 1)
                sp.wait_ge(s_ones, 2 if isinstance(n, int) and v == KEY_ITEMS - 1 else 1)
                sp.dma_start(scr["v"].rearrange("g p n -> p g n")[:, :, bass.ds(v * 2 * VCOLS, 2 * VCOLS)],
                             vst[:, place].rearrange("p g t n -> p g (t n)")).then_inc(s_vout[place], 16)

            sp.dma_start(x[:, :, :], ins["x"]).then_inc(s_x, 16)
            sp.dma_start(wk[:, :], ins["wk"]).then_inc(s_w, 16)
            sp.dma_start(mask_in[:, :], ins["mask_col"]).then_inc(s_mask, 16)
            sp.dma_start(ident[:, :], ins["ident"]).then_inc(s_x, 16)
            for n in range(RING):
                load_context(n, n)
            for i, tiles in enumerate(TABLE_TILES):
                sp.dma_start(cos_k[:, tiles, :], ins["cos_k"][:, tiles, :]).then_inc(s_tab[i], 16)
                sp.dma_start(sin_k[:, tiles, :], ins["sin_k"][:, tiles, :]).then_inc(s_tab[i], 16)
            sp.dma_start(wq[:, :], ins["wq"]).then_inc(s_late, 16)
            sp.dma_start(wv[:, :], ins["wv"]).then_inc(s_late, 16)
            sp.dma_start(cos_q[:, :, :], ins["cos_q"]).then_inc(s_late, 16)
            sp.dma_start(sin_q[:, :, :], ins["sin_q"]).then_inc(s_late, 16)
            sp.dma_start(valid[:, :], ins["valid"]).then_inc(s_late, 16)
            through(sp, 0, KEY_ITEMS - RING, keys)
            for n in range(KEY_ITEMS - RING, KEY_ITEMS):
                keys(n, n % RING, n // RING)
            through(sp, KEY_ITEMS, QUERY_ITEMS, queries)
            through(sp, KEY_ITEMS, KEY_ITEMS - RING, values)
            for n in range(2 * KEY_ITEMS - RING, 2 * KEY_ITEMS):
                values(n, n % RING, n // RING)
            for place in range(RING):
                sp.wait_ge(s_out[place], 32 * len(range(place, KEY_ITEMS + QUERY_ITEMS, RING)))
                sp.wait_ge(s_vout[place], 16 * len(range((place - KEY_ITEMS) % RING, KEY_ITEMS, RING)))

        @block.tensor
        def _(pe):
            def project_keys(n, place, turn):
                pe.wait_ge(s_ctx[place], (turn + 1) * 16)
                after(pe, s_terms, n - 1)
                for t in range(2):
                    mm = pe.matmul(prod[:, place % 2, t * 256:(t + 1) * 256], ctxT[:, place, t * P:(t + 1) * P],
                                   wk[:, :], start=True, stop=True)
                mm.then_inc(s_proj, 1)

            def transpose_keys(n, place, turn):
                pe.wait_ge(s_rot, n + 1)
                after(pe, s_lo, n - 1)
                for pair in range(2):
                    for t in range(2):
                        mm = pe.transpose(turned[:, place % 2, (pair * 2 + t) * P:(pair * 2 + t + 1) * P],
                                          rot[:, place % 2, t * 256 + pair * P:t * 256 + (pair + 1) * P],
                                          ident[:, :])
                mm.then_inc(s_turn, 1)

            def project_queries(n, place, turn):
                r, half = divmod(n - KEY_ITEMS, 2)
                pe.wait_ge(s_terms, n - 1)
                pe.matmul(prod[:, place % 2, :], xT[:, r * P:(r + 1) * P], wq[:, half * 512:(half + 1) * 512],
                          start=True, stop=True).then_inc(s_proj, 1)

            def transpose_queries(n, place, turn):
                pe.wait_ge(s_rot, n + 1)
                pe.wait_ge(s_lo, n - 1)
                for pair in range(4):
                    cols = slice(pair * P, (pair + 1) * P)
                    mm = pe.transpose(turned[:, place % 2, cols], rot[:, place % 2, cols], ident[:, :])
                mm.then_inc(s_turn, 1)

            def project_values(n, place, turn):
                pe.wait_ge(s_ctx[place], (turn + 1) * 16)
                after(pe, s_vl, n - KEY_ITEMS - 1)
                for t in range(2):
                    mm = pe.matmul(v_ps[:, place % 2, t * 256:(t + 1) * 256], ctxT[:, place, t * P:(t + 1) * P],
                                   wv[:, :], start=True, stop=True)
                mm.then_inc(s_v, 1)

            pe.wait_ge(s_w, 16)
            pe.wait_ge(s_x, 32)
            through(pe, 0, KEY_ITEMS, project_keys, 1, transpose_keys)
            pe.wait_ge(s_ln, 9)
            for r in range(ROWS // P):
                pe.transpose(x_ps[:, r // 4, r % 4, :], xc[:, r, :], ident[:, :]).then_inc(s_xT, 1)
            pe.wait_ge(s_late, 16 * 5)
            pe.wait_ge(s_xTs, 2)
            pe.wait_ge(s_bnd, 4)
            pe.matmul(x_ps[:, 0, 0, 0:1], ones[:, :], bound[:, 2:3], start=True, stop=True).then_inc(s_bmm, 1)
            through(pe, KEY_ITEMS, QUERY_ITEMS, project_queries, 1, transpose_queries)
            pe.wait_ge(s_bnd, 9)
            through(pe, KEY_ITEMS, KEY_ITEMS, project_values)

        @block.vector
        def _(dve):
            def terms(n, place, shape, cos, sin):
                dve.wait_ge(s_proj, n + 1)
                after(dve, s_rot, n - 1)
                def view(t):
                    if len(shape) == 3:
                        return t.rearrange("p (h n) -> p h n", n=D)
                    return t.rearrange("p (t g n) -> p t g n", g=GROUPS, n=D)
                src, to = view(prod[:, place % 2, :]), view(t_sin[:, place % 2, :])
                dve.tensor_tensor(view(t_cos[:, place % 2, :]), src, cos.to_broadcast(shape), ALU.mult)
                half = shape[:-1] + [D // 2]
                lead = (slice(None),) * (len(shape) - 1)
                for a, b in ((0, 1), (1, 0)):
                    at = lead + (slice(a * D // 2, (a + 1) * D // 2),)
                    other = lead + (slice(b * D // 2, (b + 1) * D // 2),)
                    mm = dve.tensor_tensor(to[at], src[other], sin[at].to_broadcast(half), ALU.mult)
                mm.then_inc(s_terms, 1)

            def mask_tables(i):
                tiles = TABLE_TILES[i]
                dve.wait_ge(s_tab[i], 32)
                for tab in (cos_k, sin_k):
                    dve.tensor_tensor(tab[:, tiles, :], tab[:, tiles, :], maskf[:, tiles].unsqueeze(2).to_broadcast(
                        [P, tiles.stop - tiles.start, D]), ALU.mult).then_inc(s_masked, 1)
                dve.wait_ge(s_masked, 2 * i + 2)

            def take_largest(count, turn):
                dve.wait_ge(s_big, count)
                dve.wait_ge(s_run, turn + 1)
                dve.tensor_tensor(largest[:, :], largest[:, :], fresh[:, :], ALU.max).then_inc(s_run, 1)

            def key_terms(n, place, turn):
                if isinstance(n, int) and 2 * n in (0, FIRST_TILES - 2):
                    mask_tables(min(n, 1))
                tiles = bass.ds(n * 2, 2)
                terms(n, place, [P, 2, GROUPS, D], cos_k[:, tiles, :].unsqueeze(2), sin_k[:, tiles, :].unsqueeze(2))
                dve.wait_ge(s_ctx[place], (turn + 1) * 16)
                if place == 0:
                    dve.wait_ge(s_run, turn + 1)
                dve.tensor_reduce(fresh[:, place:place + 1], ctxT[:, place, :], AX.X, ALU.max,
                                  apply_absolute_value=True).then_inc(s_big, 1)
                if place == RING - 1:
                    take_largest(n + 1, turn)

            def query_terms(n, place, turn):
                r, half = divmod(n - KEY_ITEMS, 2)
                terms(n, place, [P, HEADS // 2, D], cos_q[:, r:r + 1, :], sin_q[:, r:r + 1, :])

            def low(n, place, turn):
                dve.wait_ge(s_hi, n + 1)
                dve.tensor_tensor(parts[:, place, 1, :], turned[:, place % 2, :],
                                  parts[:, place, 0, :].bitcast(F32), ALU.subtract).then_inc(s_lo, 1)

            def value_low(n, place, turn):
                v = n - KEY_ITEMS
                dve.wait_ge(s_vh, v + 1)
                src = v_ps[:, place % 2, :].rearrange("p (t g n) -> p g t n", t=2, n=D)
                dve.tensor_tensor(vst[:, place, :, :, D:2 * D], src, vst[:, place, :, :, 0:D], ALU.subtract
                                  ).then_inc(s_vl, 1)

            dve.memset(largest[:, :], 0.0).then_inc(s_run, 1)
            dve.memset(ones[:, :], 1.0)
            dve.wait_ge(s_x, 32)
            layer_norm(dve, None, x[:, :, :], xc[:, :, :], sq[:, :, :], st, s_ln, s_sqrt, 0, 0,
                       float(D) ** -0.5, "dve")
            dve.wait_ge(s_mask, 16)
            dve.tensor_copy(maskf[:, :], mask_in[:, :]).then_inc(s_maskf, 1)
            dve.wait_ge(s_maskf, 1)
            through(dve, 0, KEY_ITEMS, key_terms, 2, low)
            for half in range(2):
                dve.wait_ge(s_xT, 4 * (half + 1))
                dve.tensor_copy(xT[:, half * 512:(half + 1) * 512].rearrange("p (r n) -> p r n", r=4),
                                x_ps[:, half]).then_inc(s_xTs, 1)
            dve.wait_ge(s_late, 16 * 5)
            take_largest(KEY_ITEMS, KEY_ITEMS // RING)
            dve.wait_ge(s_run, KEY_ITEMS // RING + 2)
            dve.tensor_reduce(bound[:, 0:1], largest[:, :], AX.X, ALU.max).then_inc(s_bnd, 1)
            dve.tensor_reduce(bound[:, 1:2], wv[:, :], AX.X, ALU.max, apply_absolute_value=True
                              ).then_inc(s_bnd, 1)
            dve.wait_ge(s_bnd, 2)
            dve.tensor_tensor(bound[:, 2:3], bound[:, 0:1], bound[:, 1:2], ALU.mult).then_inc(s_bnd, 2)
            through(dve, KEY_ITEMS, QUERY_ITEMS, query_terms, 2, low)
            dve.wait_ge(s_bmm, 1)
            dve.tensor_scalar(bound[:, 3:4], x_ps[:, 0, 0, 0:1], 2.0 ** -100, None, ALU.max).then_inc(s_bnd, 1)
            dve.wait_ge(s_bnd, 5)
            dve.tensor_scalar(bound[:, 4:5].bitcast(I32), bound[:, 3:4].bitcast(I32), 0x7F800000, None,
                              ALU.bitwise_and).then_inc(s_bnd, 1)
            dve.wait_ge(s_bnd, 6)
            dve.tensor_scalar(bound[:, 5:6], bound[:, 4:5], 2.0 ** -14, None, ALU.mult).then_inc(s_bnd, 1)
            dve.wait_ge(s_bnd, 7)
            dve.reciprocal(v_scale[:, :], bound[:, 5:6]).then_inc(s_bnd, 1)
            dve.wait_ge(s_bnd, 8)
            dve.tensor_scalar(wv[:, :], wv[:, :], v_scale[:, :], None, ALU.mult).then_inc(s_bnd, 1)
            through(dve, KEY_ITEMS, KEY_ITEMS, value_low)

        @block.scalar
        def _(act):
            def high(n, place, turn):
                act.wait_ge(s_turn, n + 1)
                after(act, s_out[place], turn * 32)
                act.activation(parts[:, place, 0, :], turned[:, place % 2, :], ACT.Copy).then_inc(s_hi, 1)

            def value_high(n, place, turn):
                v = n - KEY_ITEMS
                act.wait_ge(s_v, v + 1)
                before = turn - KEY_ITEMS // RING - (place < KEY_ITEMS % RING)
                after(act, s_vout[place], before * 16)
                src = v_ps[:, place % 2, :].rearrange("p (t g n) -> p g t n", t=2, n=D)
                act.activation(vst[:, place, :, :, 0:D], src, ACT.Copy).then_inc(s_vh, 1)

            layer_norm(None, act, x[:, :, :], xc[:, :, :], sq[:, :, :], st, s_ln, s_sqrt, 0, 0, 1.0, "act")
            through(act, 0, KEY_ITEMS, high)
            through(act, KEY_ITEMS, QUERY_ITEMS, high)
            through(act, KEY_ITEMS, KEY_ITEMS, value_high)

        @block.gpsimd
        def _(pool):
            def rotate(n, place, turn):
                pool.wait_ge(s_terms, n + 1)
                after(pool, s_turn, n - 1)
                pool.tensor_tensor(rot[:, place % 2, :], t_cos[:, place % 2, :], t_sin[:, place % 2, :], ALU.add
                                   ).then_inc(s_rot, 1)

            pool.memset(vst[:, :, :, :, ONES], 1.0).then_inc(s_ones, 1)
            through(pool, 0, KEY_ITEMS, rotate)
            through(pool, KEY_ITEMS, QUERY_ITEMS, rotate)
            pool.wait_ge(s_late, 16 * 5)
            last = (2 * KEY_ITEMS - 1) % RING
            pool.wait_ge(s_vout[last], 16 * ((KEY_ITEMS - 1) // RING))
            for g in range(GROUPS):
                mm = pool.tensor_copy(vst[:, last, g, :, ONES], valid[:, :])
            mm.then_inc(s_ones, 1)


def attend(nc, ins, scr, v_scale, attn, den):
    with ExitStack() as ctx:
        def sb(name, shape, dt):
            return ctx.enter_context(nc.sbuf_tensor(name, shape, dt))

        def sem(name):
            return ctx.enter_context(nc.semaphore(name))

        kcols = TILES * P
        k_hilo = sb("k_hilo", [P, kcols], F32R)
        k_high = sb("k_high", [P, kcols], F32R)
        k_seek = sb("k_seek", [P, kcols], F32R)
        values = sb("values", [P, TILES, VCOLS], F16)
        table = sb("table", [P, 2, TABLE], F32)
        q_hihi = sb("q_hihi", [P, HALVES, UNIT], F32R)
        q_low = sb("q_low", [P, HALVES, UNIT], F32R)
        q_seek = sb("q_seek", [P, HALVES, UNIT], F32R)
        prob = sb("prob", [P, P_BUFS, UNIT], F32)
        prob_lo = sb("prob_lo", [P, P_BUFS, UNIT], BF16)
        seen = sb("seen", [P, A_BUFS, PIECE], BF16)
        best = sb("best", [P, BLOCKS, PIECE], BF16)
        top = sb("top", [P, 2, BLOCKS], F32)
        negmax = sb("negmax", [P, BLOCKS, P], F32R)
        ident = sb("aident", [P, P], F32)
        ident_r = sb("ident_r", [P, P], F32R)
        row_const = sb("row_const", [P, 3], F32)
        mask_row = sb("mask_row", [P, kcols], U8)
        mask_col = sb("mask_col", [P, ALL_TILES], U8)
        keep = sb("keep", [P, TILES], F32)
        drop = sb("drop", [P, TILES], F32)
        last_bias = sb("last_bias", [P, HEADS], F32)
        far = sb("far", [P, HALVES, TILES], F32)
        far_one = sb("far_one", [P, HALVES], F32)
        o_sb = sb("o_sb", [P, HALVES, BLOCKS, VCOLS], F32)

        s_ps = ctx.enter_context(nc.psum_tensor("s_ps", [P, S_BUFS, 512], F32))
        a_ps = ctx.enter_context(nc.psum_tensor("a_ps", [P, A_BUFS, 512], F32))
        o_ps = ctx.enter_context(nc.psum_tensor("o_ps", [P, 2, 512], F32))

        s_c = sem("a_c")
        s_set = sem("a_set")
        s_ks = [sem(f"a_ks{c}") for c in range(LOADS)]
        s_k = [sem(f"a_k{c}") for c in range(LOADS)]
        s_val = [sem(f"a_val{c}") for c in range(LOADS)]
        s_qs = [sem("a_qs0"), sem("a_qs1")]
        s_q = [sem("a_q0"), sem("a_q1")]
        s_far = sem("a_far")
        s_tab = sem("a_tab")
        s_seek = sem("a_seek")
        s_add = sem("a_add")
        s_copy = sem("a_copy")
        s_best = sem("a_best")
        s_after = sem("a_after")
        s_row = sem("a_row")
        s_max = sem("a_max")
        s_sc = sem("a_sc")
        s_band = sem("a_band")
        s_exp = sem("a_exp")
        s_lo = sem("a_lo")
        s_plo = sem("a_plo")
        s_pv = sem("a_pv")
        s_o = sem("a_o")
        s_osum = sem("a_osum")

        prob_hi = prob[:, :, :].bitcast(BF16).rearrange("p s (n two) -> p s n two", two=2)

        def after(eng, sem_, value):
            if not isinstance(value, int) or value > 0:
                eng.wait_ge(sem_, value)

        def half_of(s):
            return s // TILES, s % TILES

        def ahead(h, s):
            return (h, s + LAG) if s + LAG < STEPS else (h + 1, s + LAG - STEPS)

        def unit(h, u):
            return h * 2 + u

        def copies_upto(h, u, k):
            return h * sum(COPIES) + u * COPIES[0] + sum(i not in NEAR[u] for i in range(k + 1))

        def adds_upto(h, u, k):
            return h * BAND_ADDS + u * len(NEAR[0]) + sum(i in NEAR[u] for i in range(k + 1))

        BAND_ADDS = sum(map(len, NEAR))

        def read(eng, h, u, k):
            if k in NEAR[u]:
                eng.wait_ge(s_add, adds_upto(h, u, k))
            else:
                eng.wait_ge(s_copy, copies_upto(h, u, k))

        def join(k):
            r, c = divmod(k, PIECES)
            return r * (PIECES - 1) + c - 1

        block = ctx.enter_context(nc.Block())

        @block.sync
        def _(sp):
            def key_cols(c):
                return slice(c * LOAD, min((c + 1) * LOAD, kcols))

            def load_seek_keys(g, searched):
                for c in range(LOADS):
                    if searched is not None:
                        sp.wait_ge(s_seek, searched + min(2 * c + 2, PIECES))
                    sp.dma_start(k_seek[0:D, key_cols(c)].bitcast(F32),
                                 scr["k"][0, bass.ds(g * D, D), key_cols(c)]).then_inc(s_ks[c], 16)

            def load_keys(g, before):
                for c in range(LOADS):
                    lo, hi = c * LOAD_TILES, min((c + 1) * LOAD_TILES, TILES)
                    if before is not None:
                        sp.wait_ge(s_sc, before + hi)
                    for part, to in enumerate((k_hilo[0:D, key_cols(c)], k_hilo[D:P, key_cols(c)])):
                        sp.dma_start(to.bitcast(F32), scr["k"][part, bass.ds(g * D, D), key_cols(c)]
                                     ).then_inc(s_k[c], 16)
                    sp.dma_start(k_high[0:D, key_cols(c)].bitcast(F32), scr["k"][0, bass.ds(g * D, D), key_cols(c)]
                                 ).then_inc(s_k[c], 16)
                    if before is not None:
                        sp.wait_ge(s_pv, before + hi)
                    sp.dma_start(values[:, lo:hi, :],
                                 scr["v"][g, :, lo * VCOLS:hi * VCOLS].rearrange("p (t n) -> p t n", n=VCOLS)
                                 ).then_inc(s_val[c], 16)

            def query(h, part, u):
                return scr["q"][part, bass.ds(h * D, D), u * UNIT:(u + 1) * UNIT]

            def load_seek(h, u):
                sp.dma_start(q_seek[0:D, u, :].bitcast(F32), query(h, 0, u)).then_inc(s_qs[u], 16)

            def load_query(h, u):
                sp.dma_start(q_hihi[0:D, u, :].bitcast(F32), query(h, 0, u)).then_inc(s_q[u], 16)
                sp.dma_start(q_hihi[D:P, u, :].bitcast(F32), query(h, 0, u)).then_inc(s_q[u], 16)
                sp.dma_start(q_low[0:D, u, :].bitcast(F32), query(h, 1, u)).then_inc(s_q[u], 16)

            def load_table(h, b):
                sp.dma_start(table[:, b, :], ins["bias_rows"](h)).then_inc(s_tab, 16)

            def load_head(h, new_group):
                sp.wait_ge(s_seek, (h * 2 - 1) * SEEKS)
                load_seek(h, 0)
                sp.wait_ge(s_pv, (h - 1) * STEPS + 1)
                load_table(h, h % 2)
                if new_group is not None:
                    load_seek_keys(new_group, h * 2 * SEEKS - PIECES)
                sp.wait_ge(s_seek, h * 2 * SEEKS)
                load_seek(h, 1)
                sp.wait_ge(s_sc, h * STEPS - TILES)
                load_query(h, 0)
                if new_group is not None:
                    load_keys(new_group, h * STEPS - TILES)
                sp.wait_ge(s_sc, h * STEPS)
                load_query(h, 1)

            sp.dma_start(mask_row[:, :],
                         ins["mask_row"][:, 0:kcols].to_broadcast([P, kcols])).then_inc(s_c, 16)
            sp.dma_start(row_const[:, :], ins["row_const"]).then_inc(s_c, 16)
            load_seek_keys(0, None)
            load_seek(0, 0)
            sp.dma_start(ident[:, :], ins["ident"]).then_inc(s_c, 16)
            sp.dma_start(mask_col[:, :], ins["mask_col"]).then_inc(s_c, 16)
            sp.dma_start(last_bias[:, :], ins["last_bias"].to_broadcast([P, HEADS])).then_inc(s_c, 16)
            load_table(0, 0)
            load_query(0, 0)
            load_seek(0, 1)
            load_keys(0, None)
            load_query(0, 1)
            with sp.Fori(0, GROUPS - 1) as g:
                with sp.Fori(1, REP) as r:
                    load_head(g * REP + r, None)
                load_head(g * REP + REP, g + 1)
            with sp.Fori(HEADS - REP + 1, HEADS) as h:
                load_head(h, None)

        def first_search(seek):
            for j in range(TILES):
                seek(0, 0, j)

        def through_heads(eng, slot):
            for s in range(TURN):
                slot(0, s, True)
            with eng.Fori(0, HEADS - 1) as h:
                for s in range(TURN, STEPS):
                    slot(h, s, True)
                for s in range(TURN):
                    slot(h + 1, s, True)
            for s in range(TURN, STEPS):
                slot(HEADS - 1, s, False)

        def searched(h, s, more):
            u, j = half_of(s)
            if u == 0:
                return h, 1, j
            return (h + 1, 0, j) if more else None

        @block.tensor
        def _(pe):
            def seek(h, u, j, groups):
                for k in SEEK_AT.get(j, []):
                    r, c = divmod(k, PIECES)
                    if k == 0:
                        pe.wait_ge(s_qs[u], (h + 1) * 16)
                        after(pe, s_max, unit(h, u))
                    if u == 0 and r == 0 and c % 2 == 0:
                        pe.wait_ge(s_ks[c // 2], groups * 16)
                    if k >= A_BUFS:
                        read(pe, h, u, k - A_BUFS)
                    w = piece_width(c)
                    pe.matmul(a_ps[:, k % A_BUFS, 0:w], q_seek[:, u, r * P:(r + 1) * P],
                              k_seek[:, c * PIECE:c * PIECE + w], start=True, stop=True).then_inc(s_seek, 1)
                if j == ROW_STEP:
                    pe.wait_ge(s_after, (unit(h, u) + 1) * AFTER_STEPS)
                    for k in range(SEEKS - A_BUFS, SEEKS):
                        read(pe, h, u, k)
                    for r in range(BLOCKS):
                        mm = pe.matmul(a_ps[:, 0, r * P:(r + 1) * P], negmax[:, r, :], ident_r[:, :],
                                       start=True, stop=True)
                    mm.then_inc(s_row, 1)

            def scores(h, s):
                u, t = half_of(s)
                if t == 0:
                    pe.wait_ge(s_q[u], (h + 1) * 48)
                    pe.wait_ge(s_max, unit(h, u) + 1)
                after(pe, s_exp, h * STEPS + s - S_BUFS + 1)
                cols = slice(t * P, (t + 1) * P)
                pe.matmul(s_ps[:, s % S_BUFS, :], k_hilo[:, cols], q_hihi[:, u, :], start=True, stop=False)
                pe.matmul(s_ps[:, s % S_BUFS, :], k_high[:, cols], q_low[:, u, :], start=False, stop=True
                          ).then_inc(s_sc, 1)

            def products(h, s, groups):
                u, t = half_of(s)
                if t in POOL_TILES:
                    pe.wait_ge(s_plo, unit(h, u) * len(POOL_TILES) + POOL_TILES.index(t) + 1)
                else:
                    pe.wait_ge(s_lo, unit(h, u) * (TILES - len(POOL_TILES)) + t + 1 - sum(p < t for p in POOL_TILES))
                if t == 0:
                    after(pe, s_o, unit(h, u))
                if u == 0 and t % LOAD_TILES == 0:
                    pe.wait_ge(s_val[t // LOAD_TILES], groups * 16)
                for r in range(BLOCKS):
                    rows = slice(r * P, (r + 1) * P)
                    acc = o_ps[:, r // 2, (r % 2) * VCOLS:(r % 2 + 1) * VCOLS]
                    pe.matmul(acc, prob_hi[:, s % P_BUFS, rows, 1], values[:, t, :],
                              start=(t == 0 and r % 2 == 0), stop=False, skip_group_check=True)
                    mm = pe.matmul(acc, prob_lo[:, s % P_BUFS, rows], values[:, t, :],
                                   start=False, stop=(t == TILES - 1), skip_group_check=True)
                mm.then_inc(s_pv, 1)

            def slot(h, s, more, groups, next_groups):
                h2, s2 = ahead(h, s)
                if s + LAG < STEPS or more:
                    u, t = half_of(s2)
                    if u == 0 and t % LOAD_TILES == 0:
                        pe.wait_ge(s_k[t // LOAD_TILES], (groups if s + LAG < STEPS else next_groups) * 48)
                    scores(h2, s2)
                nxt = searched(h, s, more)
                if nxt:
                    seek(*nxt, groups if s < TILES else next_groups)
                products(h, s, groups)

            def turn(h, more, groups, next_groups, after_next):
                for s in range(TURN, STEPS):
                    slot(h, s, more, groups, next_groups)
                if more:
                    for s in range(TURN):
                        slot(h + 1, s, True, next_groups, after_next)

            pe.wait_ge(s_set, 8)
            for j in range(TILES):
                seek(0, 0, j, 1)
            pe.wait_ge(s_k[0], 48)
            for s in range(LAG):
                scores(0, s)
            for s in range(TURN):
                slot(0, s, True, 1, 1)
            with pe.Fori(0, GROUPS - 1) as g:
                with pe.Fori(0, REP - 1) as r:
                    turn(g * REP + r, True, g + 1, g + 1, g + 1)
                turn(g * REP + (REP - 1), True, g + 1, g + 2, g + 2)
            with pe.Fori(HEADS - REP, HEADS - 1) as h:
                turn(h, True, GROUPS, GROUPS, GROUPS)
            turn(HEADS - 1, False, GROUPS, GROUPS, GROUPS)

        @block.scalar
        def _(act):
            def seek(h, u, j):
                for k in SEEK_AT.get(j, []):
                    if k in NEAR[u]:
                        continue
                    r, c = divmod(k, PIECES)
                    act.wait_ge(s_seek, unit(h, u) * SEEKS + k + 1)
                    w = piece_width(c)
                    if c == 0:
                        to = best[:, r, :]
                        if k == 0:
                            after(act, s_after, unit(h, u) * AFTER_STEPS)
                    else:
                        to = seen[:, join(k) % A_BUFS, 0:w]
                        after(act, s_best, unit(h, u) * JOINS + join(k) - A_BUFS + 1)
                    act.activation(to, a_ps[:, k % A_BUFS, 0:w], ACT.Copy).then_inc(s_copy, 1)
                if j == ROW_STEP + 1:
                    act.wait_ge(s_row, unit(h, u) + 1)
                    act.activation(q_low[D:P, u, :], a_ps[D:P, 0, :], ACT.Copy).then_inc(s_max, 1)

            def exponentials(h, s):
                u, t = half_of(s)
                if t == 0:
                    act.wait_ge(s_far, unit(h, u) * 2 + 2)
                if t in BAND[u]:
                    done = len(BAND[0]) * u + BAND[u].index(t) + 1
                    act.wait_ge(s_band, h * BAND_PER_HEAD + done)
                    bias = drop[:, t:t + 1]
                else:
                    act.wait_ge(s_sc, h * STEPS + s + 1)
                    bias = far[:, u, t:t + 1]
                after(act, s_pv, h * STEPS + s - P_BUFS + 1)
                act.activation(prob[:, s % P_BUFS, :], s_ps[:, s % S_BUFS, :], ACT.Exp, bias=bias
                               ).then_inc(s_exp, 1)

            def take_sums(h, u):
                act.wait_ge(s_pv, h * STEPS + (u + 1) * TILES)
                act.activation(o_sb[:, u, :, :].rearrange("p (a b) n -> p a (b n)", b=2),
                               o_ps[:, :, 0:2 * VCOLS], ACT.Copy).then_inc(s_o, 1)

            def slot(h, s, more):
                if s + LAG < STEPS or more:
                    exponentials(*ahead(h, s))
                if s in (TILES - 1, STEPS - 1):
                    take_sums(h, s // TILES)
                nxt = searched(h, s, more)
                if nxt:
                    seek(*nxt)

            act.wait_ge(s_set, 8)
            first_search(seek)
            for s in range(LAG):
                exponentials(0, s)
            through_heads(act, slot)

        @block.vector
        def _(dve):
            def bias_of(h, first, w):
                return table[:, bass.ds(h % 2, 1), first:first + w].rearrange("p o n -> p (o n)")

            def add_near(h, u, k):
                r, c = divmod(k, PIECES)
                dve.wait_ge(s_seek, unit(h, u) * SEEKS + k + 1)
                w = piece_width(c)
                if c == 0:
                    to = best[:, r, :]
                else:
                    to = seen[:, join(k) % A_BUFS, :]
                    after(dve, s_best, unit(h, u) * JOINS + join(k) - A_BUFS + 1)
                dve.scalar_tensor_tensor(
                    out=to[:, 0:w], in0=bias_of(h, c * PIECE + u * UNIT + r * P, w),
                    scalar=far_one[:, u:u + 1], in1=a_ps[:, k % A_BUFS, 0:w], op0=ALU.subtract, op1=ALU.add
                ).then_inc(s_add, 1)

            def take_best(h, u, k):
                r, c = divmod(k, PIECES)
                if c == 0:
                    return
                m = join(k)
                read(dve, h, u, k)
                if c == 1:
                    read(dve, h, u, k - 1)
                after(dve, s_best, unit(h, u) * JOINS + m)
                w = piece_width(c)
                dve.tensor_tensor(best[:, r, 0:w], best[:, r, 0:w], seen[:, m % A_BUFS, 0:w], ALU.max
                                  ).then_inc(s_best, 1)

            def after_search(h, u, j):
                n = unit(h, u) * AFTER_STEPS

                def fold(i):
                    w = PIECE >> (i + 1)
                    if i == 0:
                        dve.wait_ge(s_best, (unit(h, u) + 1) * JOINS)
                    else:
                        dve.wait_ge(s_after, n + i)
                    dve.tensor_tensor(best[:, :, 0:w], best[:, :, 0:w], best[:, :, w:2 * w], ALU.max
                                      ).then_inc(s_after, 1)

                if j == FOLD_STEP:
                    fold(0)
                if j == FOLD_STEP + 1:
                    fold(1)
                    fold(2)
                    dve.wait_ge(s_after, n + FOLDS)
                    dve.tensor_reduce(top[:, 0, :], best[:, :, 0:PIECE >> FOLDS], AX.X, ALU.max
                                      ).then_inc(s_after, 1)
                if j == FOLD_STEP + 2:
                    dve.wait_ge(s_after, n + FOLDS + 1)
                    dve.tensor_scalar(top[:, 1, :], top[:, 0, :], far_one[:, u:u + 1], MASKED, ALU.add, ALU.max
                                      ).then_inc(s_after, 1)
                    dve.wait_ge(s_after, n + FOLDS + 2)
                    after(dve, s_row, unit(h, u))
                    dve.tensor_scalar(negmax[:, :, ROW_NEGMAX_HI], top[:, 1, :], -1.0, None, ALU.mult
                                      ).then_inc(s_after, 1)
                    dve.wait_ge(s_after, n + FOLDS + 3)
                    dve.scalar_tensor_tensor(out=negmax[:, :, ROW_NEGMAX_LO], in0=top[:, 1, :], scalar=-1.0,
                                             in1=negmax[:, :, ROW_NEGMAX_HI].bitcast(F32),
                                             op0=ALU.mult, op1=ALU.subtract).then_inc(s_after, 1)

            def set_far(h, u):
                n = unit(h, u) * 2
                after(dve, s_far, n)
                of_head = last_bias[:, bass.ds(h, 1)]
                dve.tensor_tensor(far_one[:, u:u + 1], of_head, of_head, ALU.max).then_inc(s_far, 1)
                dve.wait_ge(s_far, n + 1)
                dve.scalar_tensor_tensor(out=far[:, u, :], in0=keep[:, :], scalar=far_one[:, u:u + 1],
                                         in1=drop[:, :], op0=ALU.mult, op1=ALU.add).then_inc(s_far, 1)
                dve.wait_ge(s_far, n + 2)
                dve.wait_ge(s_tab, (h + 1) * 16)
                after(dve, s_after, unit(h, u) * AFTER_STEPS)

            def seek(h, u, j):
                if j == 0:
                    set_far(h, u)
                for k in SEEK_AT.get(j - 1, []):
                    take_best(h, u, k)
                for k in SEEK_AT.get(j, []):
                    if k in NEAR[u]:
                        add_near(h, u, k)
                after_search(h, u, j)

            def near_bias(h, s):
                u, t = half_of(s)
                if t in BAND[u]:
                    dve.wait_ge(s_sc, h * STEPS + s + 1)
                    dve.scalar_tensor_tensor(
                        out=s_ps[:, s % S_BUFS, :], in0=bias_of(h, t * P + u * UNIT, UNIT),
                        scalar=keep[:, t:t + 1], in1=s_ps[:, s % S_BUFS, :], op0=ALU.mult, op1=ALU.add
                    ).then_inc(s_band, 1)

            def low_part(h, s):
                u, t = half_of(s)
                if t not in POOL_TILES:
                    dve.wait_ge(s_exp, h * STEPS + s + 1)
                    dve.tensor_tensor(prob_lo[:, s % P_BUFS, :], prob[:, s % P_BUFS, :],
                                      prob_hi[:, s % P_BUFS, :, 1], ALU.subtract).then_inc(s_lo, 1)

            def slot(h, s, more):
                if s + LAG < STEPS or more:
                    near_bias(*ahead(h, s))
                if s + LAG - 1 < STEPS or more:
                    low_part(*ahead(h, s - 1))
                nxt = searched(h, s, more)
                if nxt:
                    seek(*nxt)

            dve.wait_ge(s_c, 16 * 5)
            for keys in (k_seek, k_high):
                dve.tensor_scalar(keys[D:P, :], mask_row[D:P, :], row_const[D:P, 0:1], row_const[D:P, 1:2],
                                  ALU.mult, ALU.add).then_inc(s_set, 1)
            dve.memset(prob[:, :, :], 0.0).then_inc(s_set, 1)
            dve.tensor_copy(ident_r[:, :], ident[:, :]).then_inc(s_set, 1)
            dve.tensor_copy(keep[:, :], mask_col[:, 0:TILES]).then_inc(s_set, 1)
            dve.wait_ge(s_set, 5)
            dve.tensor_scalar(q_seek[D:P, :, :], prob[D:P, 0:HALVES, :], row_const[D:P, 2:3], None, ALU.add
                              ).then_inc(s_set, 1)
            dve.tensor_copy(negmax[:, :, :], prob[:, 0, :].rearrange("p (r n) -> p r n", n=P)).then_inc(s_set, 1)
            dve.tensor_scalar(drop[:, :], keep[:, :], -MASKED, MASKED, ALU.mult, ALU.add).then_inc(s_set, 1)
            dve.wait_ge(s_set, 8)
            first_search(seek)
            for s in range(LAG):
                near_bias(0, s)
                if s < LAG - 1:
                    low_part(0, s)
            through_heads(dve, slot)

        @block.gpsimd
        def _(pool):
            def low_part(h, s):
                u, t = half_of(s)
                if t in POOL_TILES:
                    pool.wait_ge(s_exp, h * STEPS + s + 1)
                    pool.tensor_tensor(prob_lo[:, s % P_BUFS, :], prob[:, s % P_BUFS, :],
                                       prob_hi[:, s % P_BUFS, :, 1], ALU.subtract).then_inc(s_plo, 1)

            def take_output(h, u):
                pool.wait_ge(s_o, unit(h, u) + 1)
                blocks = slice(u * BLOCKS, (u + 1) * BLOCKS)
                pool.tensor_tensor(attn[:, blocks, bass.ds(h * D, D)], o_sb[:, u, :, 0:D], o_sb[:, u, :, D:2 * D],
                                   ALU.add).then_inc(s_osum, 1)
                pool.tensor_tensor(den[:, blocks, bass.ds(h, 1)], o_sb[:, u, :, ONES:ONES + 1],
                                   v_scale[:, :].unsqueeze(1).to_broadcast([P, BLOCKS, 1]), ALU.mult
                                   ).then_inc(s_osum, 1)

            def slot(h, s, more):
                if s + LAG - 1 < STEPS or more:
                    low_part(*ahead(h, s - 1))
                if s == TILES + 3:
                    take_output(h, 0)
                if s == 3 and not (isinstance(h, int) and h == 0):
                    take_output(h - 1, 1)

            through_heads(pool, slot)
            take_output(HEADS - 1, 1)



def finish(nc, ins, attn, den, out):
    with ExitStack() as ctx:
        def sb(name, shape, dt):
            return ctx.enter_context(nc.sbuf_tensor(name, shape, dt))

        def sem(name):
            return ctx.enter_context(nc.semaphore(name))

        NB = ROWS // P
        NE = HEADS * D // P
        x = sb("fx", [P, NB, DM], F32)
        x1 = sb("x1", [P, NB, DM], F32)
        xc = sb("fxc", [P, NB, DM], F32)
        sq = sb("fsq", [P, NB, DM], F32)
        st = sb("fst", [P, 4, NB], F32)
        res = sb("res", [P, NB, DM], F32)
        ident = sb("fident", [P, P], F32)
        wo = sb("wo", [P, NE, DM], F32)
        w = sb("w", [DM, 3, DM], F32)
        bias = sb("bias", [DM, 1], F32)
        attnT = sb("attnT", [P, 2, ROWS], F32)
        hT = sb("hT", [DM, 5, ROWS], F32)

        tr = ctx.enter_context(nc.psum_tensor("tr", [P, 4, 512], F32))
        acc = ctx.enter_context(nc.psum_tensor("acc", [P, 2, 512], F32))

        s_in = sem("f_in")
        s_den = sem("f_den")
        s_norm = sem("f_norm")
        s_norm2 = sem("f_norm2")
        s_tr = sem("f_tr")
        s_ev = sem("f_ev")
        s_ev2 = sem("f_ev2")
        s_acc = sem("f_acc")
        s_t = sem("f_t")
        s_y = sem("f_y")
        s_mm = sem("f_mm")
        s_ln = sem("f_ln")
        s_sqrt = sem("f_sqrt")
        s_x1 = sem("f_x1")
        s_res = sem("f_res")
        s_out = sem("f_out")

        block = ctx.enter_context(nc.Block())

        def tr_bank(i):
            return tr[:, i % 4, :]

        def normalise(eng, e, done):
            cols = attn[:, :, e * P:(e + 1) * P].rearrange("p r (h n) -> p r h n", h=2)
            eng.tensor_tensor(cols, cols, den[:, :, 2 * e:2 * e + 2].unsqueeze(3).to_broadcast([P, NB, 2, D]),
                              ALU.mult).then_inc(done, 1)

        @block.gpsimd
        def _(pool):
            pool.wait_ge(s_den, 1)
            for e in range(1, NE, 2):
                normalise(pool, e, s_norm2)

        @block.sync
        def _(sp):
            sp.dma_start(ident[:, :], ins["ident"]).then_inc(s_in, 16)
            sp.dma_start(wo[:, :, :], ins["wo"]).then_inc(s_in, 16)
            sp.dma_start(x[:, :, :], ins["x"]).then_inc(s_in, 16)
            sp.dma_start(w[:, :, :], ins["w"]).then_inc(s_in, 16)
            sp.dma_start(bias[:, :], ins["bias"]).then_inc(s_in, 16)
            for half in range(2):
                sp.wait_ge(s_res, half + 1)
                sp.dma_start(out[:, half * 4:(half + 1) * 4, :], res[:, half * 4:(half + 1) * 4, :]
                             ).then_inc(s_out, 16)
            sp.wait_ge(s_out, 32)

        @block.tensor
        def _(pe):
            pe.wait_ge(s_in, 80)
            for e in range(NE + 1):
                if e < NE:
                    pe.wait_ge((s_norm, s_norm2)[e % 2], e // 2 + 1)
                    for half in range(2):
                        if e >= 2:
                            pe.wait_ge(s_ev if half == 0 else s_ev2, e - 1)
                        for q in range(4):
                            mm = pe.transpose(tr[:, (2 * e + half) % 4, q * P:(q + 1) * P],
                                              attn[:, half * 4 + q, e * P:(e + 1) * P], ident[:, :])
                        mm.then_inc(s_tr, 1)
                if e >= 1:
                    pe.wait_ge(s_ev, e)
                    pe.wait_ge(s_ev2, e)
                    for half in range(2):
                        mm = pe.matmul(acc[:, half, :], wo[:, e - 1, :],
                                       attnT[:, (e - 1) % 2, half * 512:(half + 1) * 512],
                                       start=(e == 1), stop=(e == NE))
                    mm.then_inc(s_acc, 1)
            for half in range(2):
                pe.wait_ge(s_t, half + 1)
                for q in range(4):
                    mm = pe.transpose(tr[:, half, q * P:(q + 1) * P],
                                      hT[:, 0, (half * 4 + q) * P:(half * 4 + q + 1) * P], ident[:, :])
                mm.then_inc(s_tr, 1)
            pe.wait_ge(s_ln, 9)
            for half in range(2):
                for q in range(4):
                    mm = pe.transpose(tr[:, 2 + half, q * P:(q + 1) * P], xc[:, half * 4 + q, :], ident[:, :])
                mm.then_inc(s_tr, 1)
            for i in range(3):
                for half in range(2):
                    pe.wait_ge(s_t, 2 + 2 * i + half + 1)
                    pe.matmul(acc[:, half, :], w[:, i, :], hT[:, 1 + i, half * 512:(half + 1) * 512],
                              start=True, stop=True).then_inc(s_mm, 1)
            for half in range(2):
                pe.wait_ge(s_y, half + 1)
                for q in range(4):
                    mm = pe.transpose(tr[:, half, q * P:(q + 1) * P],
                                      hT[:, 4, (half * 4 + q) * P:(half * 4 + q + 1) * P], ident[:, :])
                mm.then_inc(s_tr, 1)

        @block.vector
        def _(dve):
            dve.reciprocal(den[:, :, :], den[:, :, :]).then_inc(s_den, 1)
            dve.wait_ge(s_den, 1)
            normalise(dve, 0, s_norm)
            dve.wait_ge(s_in, 80)
            for e in range(NE):
                if e % 2 == 0 and e + 2 < NE:
                    normalise(dve, e + 2, s_norm)
                dve.wait_ge(s_tr, 2 * e + 1)
                if e >= 2:
                    dve.wait_ge(s_acc, e - 1)
                dve.tensor_copy(attnT[:, e % 2, 0:512], tr[:, (2 * e) % 4, :]).then_inc(s_ev, 1)
            for half in range(2):
                dve.wait_ge(s_acc, NE)
                dve.tensor_copy(hT[:, 0, half * 512:(half + 1) * 512], acc[:, half, :]).then_inc(s_t, 1)
            for half in range(2):
                dve.wait_ge(s_tr, 2 * NE + half + 1)
                rows = slice(half * 4, half * 4 + 4)
                dve.tensor_tensor(x1[:, rows, :], tr[:, half, :].rearrange("p (q n) -> p q n", q=4), x[:, rows, :],
                                  ALU.add).then_inc(s_x1, 1)
            dve.wait_ge(s_x1, 2)
            layer_norm(dve, None, x1[:, :, :], xc[:, :, :], sq[:, :, :], st, s_ln, s_sqrt, 0, 0, 1.0, "dve")
            for half in range(2):
                dve.wait_ge(s_tr, 2 * NE + 2 + half + 1)
                dve.tensor_copy(hT[:, 1, half * 512:(half + 1) * 512], tr[:, 2 + half, :]).then_inc(s_t, 1)
            for i in range(2):
                for half in range(2):
                    dve.wait_ge(s_mm, 2 * i + half + 1)
                    dve.tensor_copy(hT[:, 2 + i, half * 512:(half + 1) * 512], acc[:, half, :]).then_inc(s_t, 1)
            for half in range(2):
                dve.wait_ge(s_tr, 2 * NE + 4 + half + 1)
                rows = slice(half * 4, half * 4 + 4)
                dve.tensor_tensor(res[:, rows, :], tr[:, half, :].rearrange("p (q n) -> p q n", q=4),
                                  x1[:, rows, :], ALU.add).then_inc(s_res, 1)

        @block.scalar
        def _(act):
            for e in range(NE):
                act.wait_ge(s_tr, 2 * e + 2)
                if e >= 2:
                    act.wait_ge(s_acc, e - 1)
                act.copy(attnT[:, e % 2, 512:1024], tr[:, (2 * e + 1) % 4, :]).then_inc(s_ev2, 1)
            layer_norm(None, act, x1[:, :, :], xc[:, :, :], sq[:, :, :], st, s_ln, s_sqrt, 0, 0, 1.0, "act")
            for half in range(2):
                act.wait_ge(s_mm, 4 + half + 1)
                act.activation(hT[:, 4, half * 512:(half + 1) * 512], acc[:, half, :], ACT.Tanh,
                               bias=bias[:, 0:1]).then_inc(s_y, 1)


def build(nc, aps):
    ins = dict(aps)
    ext = aps["bias_ext"]

    def bias_rows(h):
        row = ext[bass.ds(h, 1), 0:TABLE]
        return overlapped(row)

    def overlapped(row):
        return bass.AP(row.tensor, row.offset, [[1, P], [1, TABLE]])

    ins["bias_rows"] = bias_rows
    attention(nc, ins, aps["out"])


def kernel(x, ctx_1024, mask_BxS2_bf1, L0_xattn_Wq, L0_xattn_Wk, L0_xattn_Wv, L0_xattn_Wo,
           L0_xattn_rel_pos_bias, L0_ffn_weight, L0_ffn_aux_weight1, L0_ffn_aux_weight2, L0_ffn_bias):
    import numpy as np
    import concourse.bacc as bacc
    from concourse.bass_utils import run_bass_kernel_spmd

    f32 = np.float32

    xr = np.asarray(x)[0, ::-1].reshape(ROWS // P, P, DM).transpose(1, 0, 2)
    ctxT = np.zeros((DM, KEYS_PAD), f32)
    ctxT[:, :KEYS] = np.asarray(ctx_1024)[0].T
    mask = np.zeros((KEYS_PAD,), bool)
    mask[:KEYS] = np.asarray(mask_BxS2_bf1)[0]
    mask_col = mask.reshape(-1, P).T

    expo = (np.arange(0, D, 2, dtype=f32) / f32(D)).astype(np.float64)
    inv = (f32(1) / (10000.0 ** expo).astype(f32)).astype(f32)
    inv = np.repeat(inv, 2)[None, :]
    sign = np.where(np.arange(D) < D // 2, -1.0, 1.0).astype(f32)

    def rotary(fn, positions):
        angle = (inv * positions.astype(f32)[:, None]).astype(np.float64)
        return fn(angle).astype(f32).reshape(-1, P, D).transpose(1, 0, 2)

    ext = np.abs(np.arange(TABLE + P) - (ROWS - 1)).clip(0, CLIP)
    bias_ext = np.asarray(L0_xattn_rel_pos_bias)[:, ext]
    row_const = np.zeros((P, 3), f32)
    row_const[ROW_PEN, 0], row_const[ROW_PEN, 1] = PEN, -PEN
    row_const[[ROW_NEGMAX_HI, ROW_NEGMAX_LO], 1] = 1.0
    row_const[ROW_PEN, 2] = 1.0
    arrays = {
        "x": xr, "ctxT": ctxT, "mask_row": mask[None, :], "mask_col": mask_col,
        "wq": np.asarray(L0_xattn_Wq), "wk": np.asarray(L0_xattn_Wk), "wv": np.asarray(L0_xattn_Wv),
        "wo": np.asarray(L0_xattn_Wo).reshape(-1, P, DM).transpose(1, 0, 2),
        "w": np.stack([np.asarray(a) for a in (L0_ffn_weight, L0_ffn_aux_weight1, L0_ffn_aux_weight2)], axis=1),
        "bias": np.asarray(L0_ffn_bias)[:, None],
        "bias_ext": bias_ext, "last_bias": np.asarray(L0_xattn_rel_pos_bias)[:, CLIP][None, :],
        "cos_k": rotary(np.cos, np.arange(KEYS_PAD)), "sin_k": sign * rotary(np.sin, np.arange(KEYS_PAD)),
        "cos_q": rotary(np.cos, np.arange(ROWS)[::-1]), "sin_q": sign * rotary(np.sin, np.arange(ROWS)[::-1]),
        "valid": (np.arange(KEYS_PAD).reshape(-1, P).T[:, -PAD_TILES:] < KEYS).astype(f32),
        "ident": np.eye(P, dtype=f32), "row_const": row_const,
    }
    arrays = {"in_" + k: np.ascontiguousarray(v) for k, v in arrays.items()}
    nc = bacc.Bacc("TRN2", target_bir_lowering=False, num_devices=1)
    aps = {k[3:]: nc.dram_tensor(k, v.shape, mybir.dt.from_np(v.dtype), kind="ExternalInput").ap()
           for k, v in arrays.items()}
    aps["out"] = nc.dram_tensor("out", (P, ROWS // P, DM), F32, kind="ExternalOutput").ap()
    build(nc, aps)
    got = run_bass_kernel_spmd(nc, [arrays], core_ids=[0]).results[0]["out"]
    return np.ascontiguousarray(got.transpose(1, 0, 2).reshape(ROWS, DM)[::-1])[None]
```

```python
from contextlib import ExitStack

import concourse.bass as bass
from concourse import mybir

ALU = mybir.AluOpType
ACT = mybir.ActivationFunctionType
AX = mybir.AxisListType
F32 = mybir.dt.float32
F32R = mybir.dt.float32r
BF16 = mybir.dt.bfloat16
F16 = mybir.dt.float16
I32 = mybir.dt.int32
U8 = mybir.dt.uint8

P = 128
ROWS = 1024
KEYS = 6404
DM = 128
HEADS = 16
GROUPS = 4
REP = HEADS // GROUPS
D = 64
CLIP = 383
ALL_TILES = -(-KEYS // 256) * 2
KEYS_PAD = ALL_TILES * P
PAD_TILES = ALL_TILES - KEYS // P
TILES = -(-KEYS // P)
KEY_ITEMS = ALL_TILES // 2
QUERY_ITEMS = ROWS // P * 2
RING = 4
SPARE_PARTS = 6
assert TILES * P % SPARE_PARTS == 0 and 2 * SPARE_PARTS <= QUERY_ITEMS
FIRST_TILES = 12
TABLE_TILES = (slice(0, FIRST_TILES), slice(FIRST_TILES, ALL_TILES))
VALUES_AT = {}
for _v in range(KEY_ITEMS):
    VALUES_AT.setdefault(1 + _v * (QUERY_ITEMS - 1) // KEY_ITEMS, []).append(_v)
UNIT = 512
HALVES = ROWS // UNIT
BLOCKS = UNIT // P
VCOLS = 2 * D + 1
ONES = 2 * D
MASKED = -1.0e9
PEN = float(2 ** 30)
ROW_NEGMAX_HI, ROW_PEN, ROW_NEGMAX_LO = 64, 65, 96
EPS = 1e-5

PIECE = 512
PIECES = -(-KEYS // PIECE)
SEEKS = BLOCKS * PIECES
LOAD = 2 * PIECE
LOADS = -(-KEYS // LOAD)
LOAD_TILES = LOAD // P
FIRST_PIECE = 3
A_BUFS = 3
S_BUFS = 3
P_BUFS = 6
STEPS = HALVES * TILES
assert STEPS % S_BUFS == 0 and STEPS % P_BUFS == 0
PAIRED = (range(12, 32), range(62, 84))
LAG = 5


def piece_width(c):
    return min(PIECE, KEYS - c * PIECE)


def any_near(low, keys, rows):
    return low + keys - 1 + rows - 1 > ROWS - 1 - CLIP and low < ROWS - 1 + CLIP


def near_pair(half, r, c):
    return any_near(c * PIECE + half * UNIT + r * P, piece_width(c), 2 * P)


BAND = [[t for t in range(TILES) if any_near(t * P + u * UNIT, P, UNIT)] for u in range(HALVES)]
BAND_PER_HEAD = sum(map(len, BAND))
PIECE_ORDER = [(FIRST_PIECE + c) % PIECES for c in range(PIECES)]
LOAD_ORDER = list(dict.fromkeys(c // 2 for c in PIECE_ORDER))
ORDER = [(pair * 2 + b, c) for pair in range(BLOCKS // 2) for c in PIECE_ORDER for b in range(2)]
NEAR = [[i for i, (r, c) in enumerate(ORDER) if i % 2 and near_pair(u, r - 1, c)] for u in range(HALVES)]
NEAR_PER_HEAD = sum(map(len, NEAR))
JOINS = BLOCKS // 2 * (PIECES - 1)
TABLE = max([t * P + u * UNIT + UNIT for u in range(HALVES) for t in BAND[u]]
            + [ORDER[i][1] * PIECE + ORDER[i][0] * P + u * UNIT + PIECE for u in range(HALVES) for i in NEAR[u]])

SHIFT = 15
SEEK_AT = {}
for _i in range(SEEKS):
    SEEK_AT.setdefault(_i * TILES // SEEKS, []).append(_i)
FOLDS = 3
AFTER_STEPS = FOLDS + 4
ROW_STEP = TILES + 7
TURN = TILES - SHIFT
assert STEPS % 2 == 0 and TURN % 2 == 0
PE_STEPS = []
for _s in range(0, STEPS, 2):
    PE_STEPS += [(_s, _s + 1)] if any(_s in pairs for pairs in PAIRED) else [(_s,), (_s + 1,)]
ROW_PLACE = min(SEEK_AT[ROW_STEP - TILES])
ROUND_STEPS = (5, 7)
assert all(min(near) > max(SEEK_AT[ROUND_STEPS[-1] + 1]) for near in NEAR)
POOL_STEPS = [0, 2, 4, 6, 8, 50, 52, 54, 56]
LOW = []
for _s in range(0, STEPS, 2):
    LOW += [(_s, 1), (_s + 1, 1)] if _s in POOL_STEPS else [(_s, 2)]
LOW_DVE = [f for f, n in LOW if f not in POOL_STEPS]
FAR_STEP = SHIFT


def attention(nc, ins, out):
    outer = ExitStack()
    with outer:
        scr = {"k": nc.dram_tensor("k_scr", [2, GROUPS * D, KEYS_PAD], F32, kind="Internal").ap(),
               "q": nc.dram_tensor("q_scr", [2, HEADS * D, ROWS], F32, kind="Internal").ap(),
               "v": nc.dram_tensor("v_scr", [GROUPS, P, ALL_TILES * VCOLS], F16, kind="Internal").ap()}
        v_scale = outer.enter_context(nc.sbuf_tensor("v_scale", [P, 1], F32))
        keys = Keys(nc, outer)
        project(nc, ins, scr, v_scale, keys)
        attn = outer.enter_context(nc.sbuf_tensor("attn", [P, ROWS // P, HEADS * D], F32))
        den = outer.enter_context(nc.sbuf_tensor("den", [P, ROWS // P, HEADS], F32))
        attend(nc, ins, scr, v_scale, keys, attn, den)
        finish(nc, ins, attn, den, out)


class Keys:

    def __init__(self, nc, ctx):
        kcols = TILES * P
        self.hilo = ctx.enter_context(nc.sbuf_tensor("k_hilo", [P, kcols], F32R))
        self.high = ctx.enter_context(nc.sbuf_tensor("k_high", [P, kcols], F32R))
        self.seek = ctx.enter_context(nc.sbuf_tensor("k_seek", [P, kcols], F32R))
        self.s_seek = [ctx.enter_context(nc.semaphore(f"a_ks{c}")) for c in range(LOADS)]
        self.s_scores = [ctx.enter_context(nc.semaphore(f"a_k{c}")) for c in range(LOADS)]

    def cols(self, c):
        return slice(c * LOAD, min((c + 1) * LOAD, TILES * P))

    def load_seek(self, sp, scr, g, c):
        sp.dma_start(self.seek[0:D, self.cols(c)].bitcast(F32), scr["k"][0, bass.ds(g * D, D), self.cols(c)]
                     ).then_inc(self.s_seek[c], 16)

    def load_scores(self, sp, scr, g, c):
        for part, to in enumerate((self.hilo[0:D, self.cols(c)], self.hilo[D:P, self.cols(c)])):
            sp.dma_start(to.bitcast(F32), scr["k"][part, bass.ds(g * D, D), self.cols(c)]
                         ).then_inc(self.s_scores[c], 16)
        sp.dma_start(self.high[0:D, self.cols(c)].bitcast(F32), scr["k"][0, bass.ds(g * D, D), self.cols(c)]
                     ).then_inc(self.s_scores[c], 16)


def layer_norm(dve, act, x, xc, sq, st, s_dve, s_act, base_dve, base_act, factor, role):
    mean, var, sd, rs = (st[:, i, :] for i in range(4))
    wide = x.shape
    if role == "act":
        act.wait_ge(s_dve, base_dve + 6)
        act.activation(sd, var, ACT.Sqrt).then_inc(s_act, 1)
        return
    dve.tensor_reduce(mean, x, AX.X, ALU.add).then_inc(s_dve, 1)
    dve.wait_ge(s_dve, base_dve + 1)
    dve.tensor_scalar(mean, mean, -1.0 / DM, None, ALU.mult).then_inc(s_dve, 1)
    dve.wait_ge(s_dve, base_dve + 2)
    dve.tensor_tensor(xc, x, mean.unsqueeze(2).to_broadcast(wide), ALU.add).then_inc(s_dve, 1)
    dve.wait_ge(s_dve, base_dve + 3)
    dve.tensor_tensor(sq, xc, xc, ALU.mult).then_inc(s_dve, 1)
    dve.wait_ge(s_dve, base_dve + 4)
    dve.tensor_reduce(var, sq, AX.X, ALU.add).then_inc(s_dve, 1)
    dve.wait_ge(s_dve, base_dve + 5)
    dve.tensor_scalar(var, var, 1.0 / DM, EPS, ALU.mult, ALU.add).then_inc(s_dve, 1)
    dve.wait_ge(s_act, base_act + 1)
    dve.reciprocal(rs, sd).then_inc(s_dve, 1)
    dve.wait_ge(s_dve, base_dve + 7)
    dve.tensor_scalar(rs, rs, factor, None, ALU.mult).then_inc(s_dve, 1)
    dve.wait_ge(s_dve, base_dve + 8)
    dve.tensor_tensor(xc, xc, rs.unsqueeze(2).to_broadcast(wide), ALU.mult).then_inc(s_dve, 1)


def project(nc, ins, scr, v_scale, keys):
    with ExitStack() as ctx:
        def sb(name, shape, dt):
            return ctx.enter_context(nc.sbuf_tensor(name, shape, dt))

        def sem(name):
            return ctx.enter_context(nc.semaphore(name))

        x = sb("x", [P, ROWS // P, DM], F32)
        xc = sb("xc", [P, ROWS // P, DM], F32)
        sq = sb("sq", [P, ROWS // P, DM], F32)
        st = sb("st", [P, 4, ROWS // P], F32)
        xT = sb("xT", [DM, ROWS], F32)
        ident = sb("ident", [P, P], F32)
        wk = sb("wk", [DM, GROUPS * D], F32)
        wv = sb("wv", [DM, GROUPS * D], F32)
        wq = sb("wq", [DM, HEADS * D], F32)
        cos_q = sb("cos_q", [P, ROWS // P, D], F32)
        sin_q = sb("sin_q", [P, ROWS // P, D], F32)
        cos_k = sb("cos_k", [P, ALL_TILES, D], F32)
        sin_k = sb("sin_k", [P, ALL_TILES, D], F32)
        mask_in = sb("mask_in", [P, ALL_TILES], U8)
        maskf = sb("maskf", [P, ALL_TILES], F32)
        valid = sb("valid", [P, PAD_TILES], F32)
        ctxT = sb("ctxT", [DM, RING, 2 * P], F32)
        fresh = sb("fresh", [DM, RING], F32)
        largest = sb("largest", [DM, RING], F32)
        bound = sb("bound", [P, 8], F32)
        ones = sb("ones", [P, P], F32)
        t_cos = sb("t_cos", [P, 2, 512], F32)
        t_sin = sb("t_sin", [P, 2, 512], F32)
        rot = sb("rot", [P, 2, 512], F32)
        parts = sb("parts", [P, RING, 2, 512], F32R)
        vst = sb("vst", [P, RING, GROUPS, 2, VCOLS], F16)

        prod = ctx.enter_context(nc.psum_tensor("prod", [P, 2, 512], F32))
        turned = ctx.enter_context(nc.psum_tensor("turned", [P, 2, 512], F32))
        mask_row = sb("mask_row", [P, TILES * P], U8)
        row_const = sb("p_row_const", [P, 3], F32)

        v_ps = ctx.enter_context(nc.psum_tensor("v_ps", [P, 2, 512], F32))
        x_ps = ctx.enter_context(nc.psum_tensor("x_ps", [P, 2, 4, P], F32))

        s_x = sem("p_x")
        s_mask = sem("p_mask")
        s_w = sem("p_w")
        s_spare = sem("p_spare")
        s_tab = [sem("p_tab0"), sem("p_tab1")]
        s_late = sem("p_late")
        s_ctx = [sem(f"p_ctx{i}") for i in range(RING)]
        s_ln = sem("p_ln")
        s_sqrt = sem("p_sqrt")
        s_xT = sem("p_xT")
        s_xTs = sem("p_xTs")
        s_maskf = sem("p_maskf")
        s_masked = sem("p_masked")
        s_big = sem("p_big")
        s_run = sem("p_run")
        s_bnd = sem("p_bnd")
        s_bmm = sem("p_bmm")
        s_proj = sem("p_proj")
        s_terms = sem("p_terms")
        s_rot = sem("p_rot")
        s_turn = sem("p_turn")
        s_hi = sem("p_hi")
        s_lo = sem("p_lo")
        s_out = [sem(f"p_out{i}") for i in range(RING)]
        s_v = sem("p_v")
        s_vh = sem("p_vh")
        s_vl = sem("p_vl")
        s_ones = sem("p_ones")
        s_vout = [sem(f"p_vout{i}") for i in range(RING)]

        k_dst = scr["k"].rearrange("part (pair p) k -> part p pair k", p=P)
        q_dst = scr["q"].rearrange("part (pair p) k -> part p pair k", p=P)

        def after(eng, sem_, value):
            if not isinstance(value, int) or value > 0:
                eng.wait_ge(sem_, value)

        def through(eng, first, count, early, ahead=0, late=None):
            def step(n, place, turn, with_early=True, with_late=True):
                if with_early:
                    early(n, place, turn)
                if late is not None and with_late:
                    back = place - ahead
                    late(n - ahead, back % RING, turn if back >= 0 else turn - 1)

            start = first + RING + ahead
            loops = (first + count - start) // RING
            for n in range(first, start):
                step(n, n % RING, n // RING, with_late=n - ahead >= first)
            if loops:
                with eng.Fori(0, loops) as j:
                    for i in range(start, start + RING):
                        step(j * RING + i, i % RING, j + i // RING)
            for n in range(start + loops * RING, first + count + ahead):
                step(n, n % RING, n // RING, with_early=n < first + count)

        def with_values(early, ahead, late, value):
            for n in range(KEY_ITEMS, KEY_ITEMS + QUERY_ITEMS + ahead):
                if n < KEY_ITEMS + QUERY_ITEMS:
                    early(n, n % RING, n // RING)
                if late is not None and n - ahead >= KEY_ITEMS:
                    late(n - ahead, (n - ahead) % RING, (n - ahead) // RING)
                for v in VALUES_AT.get(n - KEY_ITEMS, []):
                    value(KEY_ITEMS + v, (KEY_ITEMS + v) % RING, (KEY_ITEMS + v) // RING)

        block = ctx.enter_context(nc.Block())

        @block.sync
        def _(sp):
            def load_context(n, place, v=None):
                tile = n if v is None else v
                sp.dma_start(ctxT[:, place, :], ins["ctxT"][:, bass.ds(tile * 2 * P, 2 * P)]
                             ).then_inc(s_ctx[place], 16)

            def store(n, place, dst):
                sp.wait_ge(s_lo, n + 1)
                for part in range(2):
                    sp.dma_start(dst(part), parts[:, place, part, :].bitcast(F32).rearrange(
                        "p (a n) -> p a n", n=dst(part).shape[2])).then_inc(s_out[place], 16)

            def load_tables(i):
                tiles = TABLE_TILES[i]
                sp.dma_start(cos_k[:, tiles, :], ins["cos_k"][:, tiles, :]).then_inc(s_tab[i], 16)
                sp.dma_start(sin_k[:, tiles, :], ins["sin_k"][:, tiles, :]).then_inc(s_tab[i], 16)

            def load_late():
                for to, name in ((wq[:, :], "wq"), (wv[:, :], "wv"), (cos_q[:, :, :], "cos_q"),
                                 (sin_q[:, :, :], "sin_q"), (valid[:, :], "valid")):
                    sp.dma_start(to, ins[name]).then_inc(s_late, 16)
                sp.dma_start(row_const[:, :], ins["row_const"]).then_inc(s_spare, 16)
                sp.dma_start(mask_row[D:P, :], ins["mask_row"][:, 0:TILES * P].to_broadcast([D, TILES * P])
                             ).then_inc(s_spare, 16)

            def load_keys(n, place, turn):
                i = n - KEY_ITEMS - 1
                if 0 <= i < LOADS:
                    keys.load_seek(sp, scr, 0, LOAD_ORDER[i])

            def key_item(n, place, turn):
                sp.wait_ge(s_proj, n + 1)
                sp.wait_ge(s_big, n + 1)
                if isinstance(n, int) and n + RING >= KEY_ITEMS:
                    load_context(n, place=(n + RING) % RING, v=n + RING - KEY_ITEMS)
                else:
                    load_context(n + RING, place)
                if isinstance(n, int) and n == 0:
                    load_tables(1)
                if isinstance(n, int) and n == RING - 1:
                    load_late()
                store(n, place, lambda part: k_dst[part, :, :, bass.ds(n * 2 * P, 2 * P)])

            def queries(n, place, turn):
                r, half = divmod(n - KEY_ITEMS, 2)
                store(n, place, lambda part: q_dst[part, :, half * 4:(half + 1) * 4, r * P:(r + 1) * P])

            def values(n, place, turn):
                v = n - KEY_ITEMS
                if not isinstance(n, int) or v + RING < KEY_ITEMS:
                    sp.wait_ge(s_v, v + 1)
                    load_context(n, place, v + RING)
                sp.wait_ge(s_vl, v + 1)
                sp.wait_ge(s_ones, 2 if isinstance(n, int) and v == KEY_ITEMS - 1 else 1)
                sp.dma_start(scr["v"].rearrange("g p n -> p g n")[:, :, bass.ds(v * 2 * VCOLS, 2 * VCOLS)],
                             vst[:, place].rearrange("p g t n -> p g (t n)")).then_inc(s_vout[place], 16)

            sp.dma_start(x[:, :, :], ins["x"]).then_inc(s_x, 16)
            sp.dma_start(wk[:, :], ins["wk"]).then_inc(s_w, 16)
            sp.dma_start(mask_in[:, :], ins["mask_col"]).then_inc(s_mask, 16)
            sp.dma_start(ident[:, :], ins["ident"]).then_inc(s_x, 16)
            for n in range(RING):
                load_context(n, n)
            load_tables(0)
            through(sp, 0, KEY_ITEMS - RING, key_item)
            for n in range(KEY_ITEMS - RING, KEY_ITEMS):
                key_item(n, n % RING, n // RING)
            for place in range(RING):
                sp.wait_ge(s_out[place], 32 * len(range(place, KEY_ITEMS, RING)))
            with_values(load_keys, 2, queries, values)
            for place in range(RING):
                sp.wait_ge(s_out[place], 32 * len(range(place, KEY_ITEMS + QUERY_ITEMS, RING)))
                sp.wait_ge(s_vout[place], 16 * len(range((place - KEY_ITEMS) % RING, KEY_ITEMS, RING)))

        @block.tensor
        def _(pe):
            def project_keys(n, place, turn):
                pe.wait_ge(s_ctx[place], (turn + 1) * 16)
                after(pe, s_terms, n - 1)
                for t in range(2):
                    mm = pe.matmul(prod[:, place % 2, t * 256:(t + 1) * 256], ctxT[:, place, t * P:(t + 1) * P],
                                   wk[:, :], start=True, stop=True)
                mm.then_inc(s_proj, 1)

            def transpose_keys(n, place, turn):
                pe.wait_ge(s_rot, n + 1)
                after(pe, s_lo, n - 1)
                for pair in range(2):
                    for t in range(2):
                        mm = pe.transpose(turned[:, place % 2, (pair * 2 + t) * P:(pair * 2 + t + 1) * P],
                                          rot[:, place % 2, t * 256 + pair * P:t * 256 + (pair + 1) * P],
                                          ident[:, :])
                mm.then_inc(s_turn, 1)

            def project_queries(n, place, turn):
                r, half = divmod(n - KEY_ITEMS, 2)
                pe.wait_ge(s_terms, n - 1)
                pe.matmul(prod[:, place % 2, :], xT[:, r * P:(r + 1) * P], wq[:, half * 512:(half + 1) * 512],
                          start=True, stop=True).then_inc(s_proj, 1)

            def transpose_queries(n, place, turn):
                pe.wait_ge(s_rot, n + 1)
                pe.wait_ge(s_lo, n - 1)
                for pair in range(4):
                    cols = slice(pair * P, (pair + 1) * P)
                    mm = pe.transpose(turned[:, place % 2, cols], rot[:, place % 2, cols], ident[:, :])
                mm.then_inc(s_turn, 1)

            def project_values(n, place, turn):
                if n == KEY_ITEMS:
                    pe.wait_ge(s_bnd, 9)
                pe.wait_ge(s_ctx[place], (turn + 1) * 16)
                after(pe, s_vl, n - KEY_ITEMS - 1)
                for t in range(2):
                    mm = pe.matmul(v_ps[:, place % 2, t * 256:(t + 1) * 256], ctxT[:, place, t * P:(t + 1) * P],
                                   wv[:, :], start=True, stop=True)
                mm.then_inc(s_v, 1)

            pe.wait_ge(s_w, 16)
            pe.wait_ge(s_x, 32)
            through(pe, 0, KEY_ITEMS, project_keys, 1, transpose_keys)
            pe.wait_ge(s_ln, 9)
            for r in range(ROWS // P):
                pe.transpose(x_ps[:, r // 4, r % 4, :], xc[:, r, :], ident[:, :]).then_inc(s_xT, 1)
            pe.wait_ge(s_late, 16 * 5)
            pe.wait_ge(s_xTs, 2)
            pe.wait_ge(s_bnd, 4)
            pe.matmul(x_ps[:, 0, 0, 0:1], ones[:, :], bound[:, 2:3], start=True, stop=True).then_inc(s_bmm, 1)
            with_values(project_queries, 1, transpose_queries, project_values)

        @block.vector
        def _(dve):
            def terms(n, place, shape, cos, sin):
                dve.wait_ge(s_proj, n + 1)
                after(dve, s_rot, n - 1)
                def view(t):
                    if len(shape) == 3:
                        return t.rearrange("p (h n) -> p h n", n=D)
                    return t.rearrange("p (t g n) -> p t g n", g=GROUPS, n=D)
                src, to = view(prod[:, place % 2, :]), view(t_sin[:, place % 2, :])
                dve.tensor_tensor(view(t_cos[:, place % 2, :]), src, cos.to_broadcast(shape), ALU.mult)
                half = shape[:-1] + [D // 2]
                lead = (slice(None),) * (len(shape) - 1)
                for a, b in ((0, 1), (1, 0)):
                    at = lead + (slice(a * D // 2, (a + 1) * D // 2),)
                    other = lead + (slice(b * D // 2, (b + 1) * D // 2),)
                    mm = dve.tensor_tensor(to[at], src[other], sin[at].to_broadcast(half), ALU.mult)
                mm.then_inc(s_terms, 1)

            def mask_tables(i):
                tiles = TABLE_TILES[i]
                dve.wait_ge(s_tab[i], 32)
                for tab in (cos_k, sin_k):
                    dve.tensor_tensor(tab[:, tiles, :], tab[:, tiles, :], maskf[:, tiles].unsqueeze(2).to_broadcast(
                        [P, tiles.stop - tiles.start, D]), ALU.mult).then_inc(s_masked, 1)
                dve.wait_ge(s_masked, 2 * i + 2)

            def take_largest(count, turn):
                dve.wait_ge(s_big, count)
                dve.wait_ge(s_run, turn + 1)
                dve.tensor_tensor(largest[:, :], largest[:, :], fresh[:, :], ALU.max).then_inc(s_run, 1)

            def key_terms(n, place, turn):
                if isinstance(n, int) and 2 * n in (0, FIRST_TILES - 2):
                    mask_tables(min(n, 1))
                tiles = bass.ds(n * 2, 2)
                terms(n, place, [P, 2, GROUPS, D], cos_k[:, tiles, :].unsqueeze(2), sin_k[:, tiles, :].unsqueeze(2))
                dve.wait_ge(s_ctx[place], (turn + 1) * 16)
                if place == 0:
                    dve.wait_ge(s_run, turn + 1)
                dve.tensor_reduce(fresh[:, place:place + 1], ctxT[:, place, :], AX.X, ALU.max,
                                  apply_absolute_value=True).then_inc(s_big, 1)
                if place == RING - 1:
                    take_largest(n + 1, turn)

            def query_terms(n, place, turn):
                r, half = divmod(n - KEY_ITEMS, 2)
                terms(n, place, [P, HEADS // 2, D], cos_q[:, r:r + 1, :], sin_q[:, r:r + 1, :])

            def low(n, place, turn):
                dve.wait_ge(s_hi, n + 1)
                dve.tensor_tensor(parts[:, place, 1, :], turned[:, place % 2, :],
                                  parts[:, place, 0, :].bitcast(F32), ALU.subtract).then_inc(s_lo, 1)

            def value_low(n, place, turn):
                v = n - KEY_ITEMS
                dve.wait_ge(s_vh, v + 1)
                src = v_ps[:, place % 2, :].rearrange("p (t g n) -> p g t n", t=2, n=D)
                dve.tensor_tensor(vst[:, place, :, :, D:2 * D], src, vst[:, place, :, :, 0:D], ALU.subtract
                                  ).then_inc(s_vl, 1)

            dve.memset(largest[:, :], 0.0).then_inc(s_run, 1)
            dve.memset(ones[:, :], 1.0)
            dve.wait_ge(s_x, 32)
            layer_norm(dve, None, x[:, :, :], xc[:, :, :], sq[:, :, :], st, s_ln, s_sqrt, 0, 0,
                       float(D) ** -0.5, "dve")
            dve.wait_ge(s_mask, 16)
            dve.tensor_copy(maskf[:, :], mask_in[:, :]).then_inc(s_maskf, 1)
            dve.wait_ge(s_maskf, 1)
            through(dve, 0, KEY_ITEMS, key_terms, 2, low)
            for half in range(2):
                dve.wait_ge(s_xT, 4 * (half + 1))
                dve.tensor_copy(xT[:, half * 512:(half + 1) * 512].rearrange("p (r n) -> p r n", r=4),
                                x_ps[:, half]).then_inc(s_xTs, 1)
            dve.wait_ge(s_late, 16 * 5)
            take_largest(KEY_ITEMS, KEY_ITEMS // RING)
            dve.wait_ge(s_run, KEY_ITEMS // RING + 2)
            dve.tensor_reduce(bound[:, 0:1], largest[:, :], AX.X, ALU.max).then_inc(s_bnd, 1)
            dve.tensor_reduce(bound[:, 1:2], wv[:, :], AX.X, ALU.max, apply_absolute_value=True
                              ).then_inc(s_bnd, 1)
            dve.wait_ge(s_bnd, 2)
            dve.tensor_tensor(bound[:, 2:3], bound[:, 0:1], bound[:, 1:2], ALU.mult).then_inc(s_bnd, 2)
            dve.wait_ge(s_bmm, 1)
            dve.tensor_scalar(bound[:, 3:4], x_ps[:, 0, 0, 0:1], 2.0 ** -100, None, ALU.max).then_inc(s_bnd, 1)
            dve.wait_ge(s_bnd, 5)
            dve.tensor_scalar(bound[:, 4:5].bitcast(I32), bound[:, 3:4].bitcast(I32), 0x7F800000, None,
                              ALU.bitwise_and).then_inc(s_bnd, 1)
            dve.wait_ge(s_bnd, 6)
            dve.tensor_scalar(bound[:, 5:6], bound[:, 4:5], 2.0 ** -14, None, ALU.mult).then_inc(s_bnd, 1)
            dve.wait_ge(s_bnd, 7)
            dve.reciprocal(v_scale[:, :], bound[:, 5:6]).then_inc(s_bnd, 1)
            dve.wait_ge(s_bnd, 8)
            dve.tensor_scalar(wv[:, :], wv[:, :], v_scale[:, :], None, ALU.mult).then_inc(s_bnd, 1)
            with_values(query_terms, 2, low, value_low)

        @block.scalar
        def _(act):
            def high(n, place, turn):
                act.wait_ge(s_turn, n + 1)
                after(act, s_out[place], turn * 32)
                act.activation(parts[:, place, 0, :], turned[:, place % 2, :], ACT.Copy).then_inc(s_hi, 1)

            def value_high(n, place, turn):
                v = n - KEY_ITEMS
                act.wait_ge(s_v, v + 1)
                before = turn - KEY_ITEMS // RING - (place < KEY_ITEMS % RING)
                after(act, s_vout[place], before * 16)
                src = v_ps[:, place % 2, :].rearrange("p (t g n) -> p g t n", t=2, n=D)
                act.activation(vst[:, place, :, :, 0:D], src, ACT.Copy).then_inc(s_vh, 1)

            def spare_rows(n, place, turn):
                part = n - KEY_ITEMS
                if part < 2 * SPARE_PARTS:
                    to, cols = (keys.seek, keys.high)[part // SPARE_PARTS], TILES * P // SPARE_PARTS
                    cols = slice(part % SPARE_PARTS * cols, (part % SPARE_PARTS + 1) * cols)
                    act.activation(to[D:P, cols], mask_row[D:P, cols], ACT.Identity, scale=row_const[D:P, 0:1],
                                   bias=row_const[D:P, 1:2])

            layer_norm(None, act, x[:, :, :], xc[:, :, :], sq[:, :, :], st, s_ln, s_sqrt, 0, 0, 1.0, "act")
            through(act, 0, KEY_ITEMS, high)
            act.wait_ge(s_spare, 32)
            with_values(spare_rows, 2, high, value_high)

        @block.gpsimd
        def _(pool):
            def rotate(n, place, turn):
                pool.wait_ge(s_terms, n + 1)
                after(pool, s_turn, n - 1)
                pool.tensor_tensor(rot[:, place % 2, :], t_cos[:, place % 2, :], t_sin[:, place % 2, :], ALU.add
                                   ).then_inc(s_rot, 1)

            pool.memset(vst[:, :, :, :, ONES], 1.0).then_inc(s_ones, 1)
            through(pool, 0, KEY_ITEMS, rotate)
            through(pool, KEY_ITEMS, QUERY_ITEMS, rotate)
            pool.wait_ge(s_late, 16 * 5)
            last = (2 * KEY_ITEMS - 1) % RING
            pool.wait_ge(s_vout[last], 16 * ((KEY_ITEMS - 1) // RING))
            for g in range(GROUPS):
                mm = pool.tensor_copy(vst[:, last, g, :, ONES], valid[:, :])
            mm.then_inc(s_ones, 1)


def attend(nc, ins, scr, v_scale, keys, attn, den):
    with ExitStack() as ctx:
        def sb(name, shape, dt):
            return ctx.enter_context(nc.sbuf_tensor(name, shape, dt))

        def sem(name):
            return ctx.enter_context(nc.semaphore(name))

        k_hilo, k_high, k_seek = keys.hilo, keys.high, keys.seek
        s_ks, s_k = keys.s_seek, keys.s_scores
        values = sb("values", [P, TILES, VCOLS], F16)
        table = sb("table", [P, 2, TABLE], F32)
        table_b = sb("table_b", [P, 2, TABLE], BF16)
        q_hihi = sb("q_hihi", [P, HALVES, UNIT], F32R)
        q_low = sb("q_low", [P, HALVES, UNIT], F32R)
        q_seek = sb("q_seek", [P, HALVES, UNIT], F32R)
        prob = sb("prob", [P, P_BUFS, UNIT], F32)
        prob_lo = sb("prob_lo", [P, P_BUFS, UNIT], BF16)
        seen = sb("seen", [P, 2, 2, PIECE], BF16)
        best = sb("best", [P, HALVES, BLOCKS, PIECE], BF16)
        top = sb("top", [P, 2, BLOCKS], F32)
        negmax = sb("negmax", [P, BLOCKS, P], F32R)
        ident = sb("aident", [P, P], F32)
        ident_r = sb("ident_r", [P, P], F32R)
        row_const = sb("row_const", [P, 3], F32)
        mask_col = sb("mask_col", [P, ALL_TILES], U8)
        keep = sb("keep", [P, TILES], F32)
        drop = sb("drop", [P, TILES], F32)
        last_bias = sb("last_bias", [P, HEADS], F32)
        far = sb("far", [P, HALVES, TILES], F32)
        far_one = sb("far_one", [P, HALVES], F32)
        o_sb = sb("o_sb", [P, HALVES, BLOCKS, VCOLS], F32)

        s_ps = ctx.enter_context(nc.psum_tensor("s_ps", [P, S_BUFS, 512], F32))
        a_ps = ctx.enter_context(nc.psum_tensor("a_ps", [P, A_BUFS, 512], F32))
        o_ps = ctx.enter_context(nc.psum_tensor("o_ps", [P, 2, 512], F32))

        s_c = sem("a_c")
        s_set = sem("a_set")
        s_val = [sem(f"a_val{c}") for c in range(LOADS)]
        s_qs = [sem("a_qs0"), sem("a_qs1")]
        s_q = [sem("a_q0"), sem("a_q1")]
        s_tab_b = sem("a_tab_b")
        s_one = sem("a_one")
        s_far = sem("a_far")
        s_tab = sem("a_tab")
        s_seek = sem("a_seek")
        s_copy = sem("a_copy")
        s_add = sem("a_add")
        s_best = sem("a_best")
        s_after = sem("a_after")
        s_row = sem("a_row")
        s_max = sem("a_max")
        s_sc = sem("a_sc")
        s_band = sem("a_band")
        s_exp = sem("a_exp")
        s_lo = sem("a_lo")
        s_plo = sem("a_plo")
        s_pv = sem("a_pv")
        s_o = sem("a_o")
        s_osum = sem("a_osum")

        prob_hi = prob[:, :, :].bitcast(BF16).rearrange("p s (n two) -> p s n two", two=2)

        def after(eng, sem_, value):
            if not isinstance(value, int) or value > 0:
                eng.wait_ge(sem_, value)

        def half_of(s):
            return s // TILES, s % TILES

        def ahead(h, s):
            return (h, s + LAG) if s + LAG < STEPS else (h + 1, s + LAG - STEPS)

        def unit(h, u):
            return h * 2 + u

        def read(eng, h, u, i):
            eng.wait_ge(s_copy, unit(h, u) * SEEKS + i + 1)

        def bank(i):
            return (i if i < ROW_PLACE else i + 1) % A_BUFS

        def pair_of(i):
            pair, place = divmod(i // 2, PIECES)
            return pair * (PIECES - 1) + place - 1

        block = ctx.enter_context(nc.Block())

        @block.sync
        def _(sp):
            def load_seek_keys(g, loads, searched=None):
                for c in loads:
                    if searched is not None:
                        used = max(i for i, k in enumerate(PIECE_ORDER) if k // 2 == c) + 1
                        sp.wait_ge(s_seek, searched + 2 * used)
                    keys.load_seek(sp, scr, g, c)

            def load_keys(g, before):
                for c in range(LOADS):
                    lo, hi = c * LOAD_TILES, min((c + 1) * LOAD_TILES, TILES)
                    if before is not None:
                        sp.wait_ge(s_sc, before + hi)
                    keys.load_scores(sp, scr, g, c)
                    if before is not None:
                        sp.wait_ge(s_pv, before + hi)
                    sp.dma_start(values[:, lo:hi, :],
                                 scr["v"][g, :, lo * VCOLS:hi * VCOLS].rearrange("p (t n) -> p t n", n=VCOLS)
                                 ).then_inc(s_val[c], 16)

            def query(h, part, u):
                return scr["q"][part, bass.ds(h * D, D), u * UNIT:(u + 1) * UNIT]

            def load_seek(h, u):
                sp.dma_start(q_seek[0:D, u, :].bitcast(F32), query(h, 0, u)).then_inc(s_qs[u], 16)

            def load_query(h, u):
                sp.dma_start(q_hihi[0:D, u, :].bitcast(F32), query(h, 0, u)).then_inc(s_q[u], 16)
                sp.dma_start(q_hihi[D:P, u, :].bitcast(F32), query(h, 0, u)).then_inc(s_q[u], 16)
                sp.dma_start(q_low[0:D, u, :].bitcast(F32), query(h, 1, u)).then_inc(s_q[u], 16)

            def load_table(h, b):
                sp.dma_start(table[:, b, :], ins["bias_rows"](h)).then_inc(s_tab, 16)

            def load_head(h, new_group):
                sp.wait_ge(s_seek, (h * 2 - 1) * SEEKS)
                load_seek(h, 0)
                sp.wait_ge(s_pv, (h - 1) * STEPS + 1)
                load_table(h, h % 2)
                if new_group is not None:
                    load_seek_keys(new_group, LOAD_ORDER[:-1], h * 2 * SEEKS - 2 * PIECES)
                sp.wait_ge(s_seek, h * 2 * SEEKS)
                load_seek(h, 1)
                if new_group is not None:
                    load_seek_keys(new_group, LOAD_ORDER[-1:])
                sp.wait_ge(s_sc, h * STEPS - TILES)
                load_query(h, 0)
                if new_group is not None:
                    load_keys(new_group, h * STEPS - TILES)
                sp.wait_ge(s_sc, h * STEPS)
                load_query(h, 1)

            sp.dma_start(row_const[:, :], ins["row_const"]).then_inc(s_c, 16)
            load_seek(0, 0)
            sp.dma_start(ident[:, :], ins["ident"]).then_inc(s_c, 16)
            sp.dma_start(mask_col[:, :], ins["mask_col"]).then_inc(s_c, 16)
            sp.dma_start(last_bias[:, :], ins["last_bias"].to_broadcast([P, HEADS])).then_inc(s_c, 16)
            load_table(0, 0)
            load_query(0, 0)
            load_seek(0, 1)
            load_keys(0, None)
            load_query(0, 1)
            with sp.Fori(0, GROUPS - 1) as g:
                with sp.Fori(1, REP) as r:
                    load_head(g * REP + r, None)
                load_head(g * REP + REP, g + 1)
            with sp.Fori(HEADS - REP + 1, HEADS) as h:
                load_head(h, None)

        def first_search(seek):
            for j in range(TILES):
                seek(0, 0, j)
            for j in range(SHIFT):
                seek(0, 0, TILES + j)
                seek(0, 1, j)

        def through_heads(eng, slot):
            for s in range(TURN):
                slot(0, s, True)
            with eng.Fori(0, HEADS - 1) as h:
                for s in range(TURN, STEPS):
                    slot(h, s, True)
                for s in range(TURN):
                    slot(h + 1, s, True)
            for s in range(TURN, STEPS):
                slot(HEADS - 1, s, False)

        def searched(h, s, more):
            x = s + SHIFT
            units = [(h, 0, x + TILES), (h, 1, x)]
            if more:
                units += [(h + 1, 0, x - TILES), (h + 1, 1, x - 2 * TILES)]
            return [(h2, u, j) for h2, u, j in units if 0 <= j < TILES + SHIFT]

        @block.tensor
        def _(pe):
            def seek(h, u, j, groups, followed=True):
                last = (h, 0) if u else (h - 1, 1)
                first_unit = isinstance(h, int) and h == 0 and u == 0
                for i in SEEK_AT.get(j, []):
                    r, c = ORDER[i]
                    if i == 0:
                        pe.wait_ge(s_qs[u], (h + 1) * 16)
                    if u == 0 and i < 2 * PIECES and i % 2 == 0 and c // 2 not in {
                            k // 2 for k in PIECE_ORDER[:i // 2]}:
                        pe.wait_ge(s_ks[c // 2], groups * 16)
                    if i >= A_BUFS and i != ROW_PLACE + 2:
                        read(pe, h, u, i - A_BUFS if i > ROW_PLACE + 2 or i < ROW_PLACE else i - A_BUFS + 1)
                    elif first_unit and i == ROW_PLACE + 2:
                        read(pe, h, u, ROW_PLACE - A_BUFS)
                    elif i == ROW_PLACE + 2:
                        pe.wait_ge(s_max, unit(h, u))
                    elif not first_unit:
                        read(pe, *last, SEEKS - 1 if i else SEEKS - 2)
                    w = piece_width(c)
                    pe.matmul(a_ps[:, bank(i), 0:w], q_seek[:, u, r * P:(r + 1) * P],
                              k_seek[:, c * PIECE:c * PIECE + w], start=True, stop=True).then_inc(s_seek, 1)
                if j == ROW_STEP:
                    pe.wait_ge(s_after, (unit(h, u) + 1) * AFTER_STEPS)
                    if followed:
                        read(pe, *((h + 1, 0) if u else (h, 1)), ROW_PLACE - A_BUFS)
                    for r in range(BLOCKS):
                        mm = pe.matmul(a_ps[:, ROW_PLACE % A_BUFS, r * P:(r + 1) * P], negmax[:, r, :], ident_r[:, :],
                                       start=True, stop=True)
                    mm.then_inc(s_row, 1)

            def scores(h, s):
                u, t = half_of(s)
                if t == 0:
                    pe.wait_ge(s_q[u], (h + 1) * 48)
                    pe.wait_ge(s_max, unit(h, u) + 1)
                after(pe, s_exp, h * STEPS + s - S_BUFS + 1)
                cols = slice(t * P, (t + 1) * P)
                pe.matmul(s_ps[:, s % S_BUFS, :], k_hilo[:, cols], q_hihi[:, u, :], start=True, stop=False)
                pe.matmul(s_ps[:, s % S_BUFS, :], k_high[:, cols], q_low[:, u, :], start=False, stop=True
                          ).then_inc(s_sc, 1)

            def products(h, s, groups):
                u, t = half_of(s)
                if s in POOL_STEPS:
                    pe.wait_ge(s_plo, h * len(POOL_STEPS) + POOL_STEPS.index(s) + 1)
                elif s in LOW_DVE:
                    pe.wait_ge(s_lo, h * len(LOW_DVE) + LOW_DVE.index(s) + 1)
                if t == 0:
                    after(pe, s_o, unit(h, u))
                if u == 0 and t % LOAD_TILES == 0:
                    pe.wait_ge(s_val[t // LOAD_TILES], groups * 16)
                for r in range(BLOCKS):
                    rows = slice(r * P, (r + 1) * P)
                    acc = o_ps[:, r // 2, (r % 2) * VCOLS:(r % 2 + 1) * VCOLS]
                    pe.matmul(acc, prob_hi[:, s % P_BUFS, rows, 1], values[:, t, :],
                              start=(t == 0 and r % 2 == 0), stop=False, skip_group_check=True)
                    mm = pe.matmul(acc, prob_lo[:, s % P_BUFS, rows], values[:, t, :],
                                   start=False, stop=(t == TILES - 1), skip_group_check=True)
                mm.then_inc(s_pv, 1)

            def slots(h, both, more, groups, next_groups):
                for s in both:
                    h2, s2 = ahead(h, s)
                    if s + LAG < STEPS or more:
                        u, t = half_of(s2)
                        if u == 0 and t % LOAD_TILES == 0:
                            pe.wait_ge(s_k[t // LOAD_TILES], (groups if s + LAG < STEPS else next_groups) * 48)
                        scores(h2, s2)
                for s in both:
                    for h2, u, j in searched(h, s, more):
                        seek(h2, u, j, next_groups, more or j < ROW_STEP)
                for s in both:
                    products(h, s, groups)

            def turn(h, more, groups, next_groups, after_next):
                for steps in PE_STEPS:
                    if steps[0] >= TURN:
                        slots(h, steps, more, groups, next_groups)
                for steps in PE_STEPS:
                    if steps[0] < TURN and more:
                        slots(h + 1, steps, True, next_groups, after_next)

            pe.wait_ge(s_set, 6)
            first_search(lambda h, u, j: seek(h, u, j, 1))
            pe.wait_ge(s_k[0], 48)
            for s in range(LAG):
                scores(0, s)
            for steps in PE_STEPS:
                if steps[0] < TURN:
                    slots(0, steps, True, 1, 1)
            with pe.Fori(0, GROUPS - 1) as g:
                with pe.Fori(0, REP - 1) as r:
                    turn(g * REP + r, True, g + 1, g + 1, g + 1)
                turn(g * REP + (REP - 1), True, g + 1, g + 2, g + 2)
            with pe.Fori(HEADS - REP, HEADS - 1) as h:
                turn(h, True, GROUPS, GROUPS, GROUPS)
            turn(HEADS - 1, False, GROUPS, GROUPS, GROUPS)

        @block.scalar
        def _(act):
            def seek(h, u, j):
                for i in SEEK_AT.get(j, []):
                    r, c = ORDER[i]
                    act.wait_ge(s_seek, unit(h, u) * SEEKS + i + 1)
                    w = piece_width(c)
                    if c == FIRST_PIECE:
                        to = best[:, u, r, :]
                        if i < 2:
                            after(act, s_after, (unit(h, u) - 1) * AFTER_STEPS)
                    else:
                        to = seen[:, pair_of(i) % 2, i % 2, 0:w]
                        after(act, s_best, unit(h, u) * JOINS + pair_of(i) - 1)
                    act.activation(to, a_ps[:, bank(i), 0:w], ACT.Copy).then_inc(s_copy, 1)
                if j == ROW_STEP + 1:
                    act.wait_ge(s_row, unit(h, u) + 1)
                    act.activation(q_low[D:P, u, :], a_ps[D:P, ROW_PLACE % A_BUFS, :], ACT.Copy).then_inc(s_max, 1)

            def exponentials(h, s):
                u, t = half_of(s)
                if t == 0:
                    act.wait_ge(s_far, unit(h, u) + 1)
                if t in BAND[u]:
                    done = len(BAND[0]) * u + BAND[u].index(t) + 1
                    act.wait_ge(s_band, h * BAND_PER_HEAD + done)
                    bias = drop[:, t:t + 1]
                else:
                    act.wait_ge(s_sc, h * STEPS + s + 1)
                    bias = far[:, u, t:t + 1]
                after(act, s_pv, h * STEPS + s - P_BUFS + 1)
                act.activation(prob[:, s % P_BUFS, :], s_ps[:, s % S_BUFS, :], ACT.Exp, bias=bias
                               ).then_inc(s_exp, 1)

            def take_sums(h, u):
                act.wait_ge(s_pv, h * STEPS + (u + 1) * TILES)
                act.wait_ge(s_osum, unit(h, u) * 2 + 1)
                act.activation(o_sb[:, u, :, :].rearrange("p (a b) n -> p a (b n)", b=2),
                               o_ps[:, :, 0:2 * VCOLS], ACT.Copy).then_inc(s_o, 1)

            def slot(h, s, more):
                if s in (TILES - 1, STEPS - 1):
                    take_sums(h, s // TILES)
                if s + LAG < STEPS or more:
                    exponentials(*ahead(h, s))
                for search in searched(h, s, more):
                    seek(*search)

            act.wait_ge(s_set, 6)
            first_search(seek)
            for s in range(LAG):
                exponentials(0, s)
            through_heads(act, slot)

        @block.vector
        def _(dve):
            def near_bias_of(h, first, w):
                row = table_b[:, bass.ds(h % 2, 1), first:first + w]
                return bass.AP(row.tensor, row.offset, [row.ap[0], [P, 2], [1, w]])

            def bias_of(h, first, w):
                return table[:, bass.ds(h % 2, 1), first:first + w].rearrange("p o n -> p (o n)")

            def take_best(h, u, i):
                r, c = ORDER[i - 1]
                if i % 2 == 0:
                    return
                w = piece_width(c)
                best_of = best[:, u, r:r + 2, 0:w]
                new = best_of if c == FIRST_PIECE else seen[:, pair_of(i) % 2, :, 0:w]
                read(dve, h, u, i)
                if i in NEAR[u]:
                    dve.tensor_tensor(new, new, near_bias_of(h, c * PIECE + u * UNIT + r * P, w), ALU.add
                                      ).then_inc(s_add, 1)
                if c == FIRST_PIECE:
                    return
                if c == PIECE_ORDER[1]:
                    read(dve, h, u, i - 2)
                if i in NEAR[u] or i - 2 in NEAR[u]:
                    last = max(k for k in NEAR[u] if k <= i)
                    dve.wait_ge(s_add, h * NEAR_PER_HEAD + u * len(NEAR[0]) + NEAR[u].index(last) + 1)
                after(dve, s_best, unit(h, u) * JOINS + pair_of(i))
                dve.tensor_tensor(best_of, best_of, new, ALU.max).then_inc(s_best, 1)

            def after_search(h, u, j):
                n = unit(h, u) * AFTER_STEPS

                def fold(i):
                    w = PIECE >> (i + 1)
                    if i == 0:
                        dve.wait_ge(s_best, (unit(h, u) + 1) * JOINS)
                    else:
                        dve.wait_ge(s_after, n + i)
                    dve.tensor_tensor(best[:, u, :, 0:w], best[:, u, :, 0:w], best[:, u, :, w:2 * w], ALU.max
                                      ).then_inc(s_after, 1)

                if j == TILES:
                    fold(0)
                if j == TILES + 1:
                    fold(1)
                    fold(2)
                    dve.wait_ge(s_after, n + FOLDS)
                    dve.tensor_reduce(top[:, 0, :], best[:, u, :, 0:PIECE >> FOLDS], AX.X, ALU.max
                                      ).then_inc(s_after, 1)
                if j == TILES + 2:
                    dve.wait_ge(s_after, n + FOLDS + 1)
                    dve.tensor_scalar(top[:, 1, :], top[:, 0, :], far_one[:, u:u + 1], MASKED, ALU.add, ALU.max
                                      ).then_inc(s_after, 1)
                    dve.wait_ge(s_after, n + FOLDS + 2)
                    after(dve, s_row, unit(h, u))
                    dve.tensor_scalar(negmax[:, :, ROW_NEGMAX_HI], top[:, 1, :], -1.0, None, ALU.mult
                                      ).then_inc(s_after, 1)
                    dve.wait_ge(s_after, n + FOLDS + 3)
                    dve.scalar_tensor_tensor(out=negmax[:, :, ROW_NEGMAX_LO], in0=top[:, 1, :], scalar=-1.0,
                                             in1=negmax[:, :, ROW_NEGMAX_HI].bitcast(F32),
                                             op0=ALU.mult, op1=ALU.subtract).then_inc(s_after, 1)

            def seek(h, u, j):
                if j == 0:
                    after(dve, s_after, (unit(h, u) - 1) * AFTER_STEPS)
                    dve.wait_ge(s_tab, (h + 1) * 16)
                    of_head = last_bias[:, bass.ds(h, 1)]
                    dve.tensor_tensor(far_one[:, u:u + 1], of_head, of_head, ALU.max).then_inc(s_one, 1)
                    dve.wait_ge(s_one, unit(h, u) + 1)
                if u == 0 and j in ROUND_STEPS:
                    part = ROUND_STEPS.index(j)
                    cols = slice(part * TABLE // 2, (part + 1) * TABLE // 2)
                    dve.tensor_scalar(table_b[:, bass.ds(h % 2, 1), cols], table[:, bass.ds(h % 2, 1), cols],
                                      far_one[:, 0:1], None, ALU.subtract).then_inc(s_tab_b, 1)
                if u == 0 and j == ROUND_STEPS[-1] + 1:
                    dve.wait_ge(s_tab_b, h * 2 + 2)
                if j == FAR_STEP:
                    dve.scalar_tensor_tensor(out=far[:, u, :], in0=keep[:, :], scalar=far_one[:, u:u + 1],
                                             in1=drop[:, :], op0=ALU.mult, op1=ALU.add).then_inc(s_far, 1)
                for i in SEEK_AT.get(j - 1, []):
                    take_best(h, u, i)
                after_search(h, u, j)

            def near_bias(h, s):
                u, t = half_of(s)
                if t in BAND[u]:
                    dve.wait_ge(s_sc, h * STEPS + s + 1)
                    dve.scalar_tensor_tensor(
                        out=s_ps[:, s % S_BUFS, :], in0=bias_of(h, t * P + u * UNIT, UNIT),
                        scalar=keep[:, t:t + 1], in1=s_ps[:, s % S_BUFS, :], op0=ALU.mult, op1=ALU.add
                    ).then_inc(s_band, 1)

            def low_parts(h, s):
                for first, n in LOW:
                    if first + n - 1 == s and first not in POOL_STEPS:
                        bufs = slice(first % P_BUFS, first % P_BUFS + n)
                        dve.wait_ge(s_exp, h * STEPS + s + 1)
                        dve.tensor_tensor(prob_lo[:, bufs, :], prob[:, bufs, :], prob_hi[:, bufs, :, 1],
                                          ALU.subtract).then_inc(s_lo, 1)

            def slot(h, s, more):
                if s + LAG < STEPS or more:
                    near_bias(*ahead(h, s))
                if s + LAG - 1 < STEPS or more:
                    low_parts(*ahead(h, s - 1))
                for search in searched(h, s, more):
                    seek(*search)

            dve.memset(prob[:, 0:HALVES, :], 0.0).then_inc(s_set, 1)
            dve.wait_ge(s_c, 16 * 4)
            dve.tensor_copy(ident_r[:, :], ident[:, :]).then_inc(s_set, 1)
            dve.tensor_copy(keep[:, :], mask_col[:, 0:TILES]).then_inc(s_set, 1)
            dve.wait_ge(s_set, 3)
            dve.tensor_scalar(q_seek[D:P, :, :], prob[D:P, 0:HALVES, :], row_const[D:P, 2:3], None, ALU.add
                              ).then_inc(s_set, 1)
            dve.tensor_copy(negmax[:, :, :], prob[:, 0, :].rearrange("p (r n) -> p r n", n=P)).then_inc(s_set, 1)
            dve.tensor_scalar(drop[:, :], keep[:, :], -MASKED, MASKED, ALU.mult, ALU.add).then_inc(s_set, 1)
            dve.wait_ge(s_set, 6)
            first_search(seek)
            for s in range(LAG):
                near_bias(0, s)
                if s < LAG - 1:
                    low_parts(0, s)
            through_heads(dve, slot)

        @block.gpsimd
        def _(pool):
            def take_output(h, u):
                pool.wait_ge(s_o, unit(h, u) + 1)
                blocks = slice(u * BLOCKS, (u + 1) * BLOCKS)
                pool.tensor_tensor(attn[:, blocks, bass.ds(h * D, D)], o_sb[:, u, :, 0:D], o_sb[:, u, :, D:2 * D],
                                   ALU.add).then_inc(s_osum, 1)
                pool.tensor_tensor(den[:, blocks, bass.ds(h, 1)], o_sb[:, u, :, ONES:ONES + 1],
                                   v_scale[:, :].unsqueeze(1).to_broadcast([P, BLOCKS, 1]), ALU.mult
                                   ).then_inc(s_osum, 1)

            def low_part(h, s):
                if s in POOL_STEPS:
                    pool.wait_ge(s_exp, h * STEPS + s + 1)
                    pool.tensor_tensor(prob_lo[:, s % P_BUFS, :], prob[:, s % P_BUFS, :],
                                       prob_hi[:, s % P_BUFS, :, 1], ALU.subtract).then_inc(s_plo, 1)

            def slot(h, s, more):
                if s + LAG < STEPS or more:
                    low_part(*ahead(h, s))
                if s == TILES + 3:
                    take_output(h, 0)
                if s == 3 and not (isinstance(h, int) and h == 0):
                    take_output(h - 1, 1)

            pool.memset(den[:, :, :], 0.0).then_inc(s_osum, 1)
            for s in range(LAG):
                low_part(0, s)
            through_heads(pool, slot)
            take_output(HEADS - 1, 1)



def finish(nc, ins, attn, den, out):
    with ExitStack() as ctx:
        def sb(name, shape, dt):
            return ctx.enter_context(nc.sbuf_tensor(name, shape, dt))

        def sem(name):
            return ctx.enter_context(nc.semaphore(name))

        NB = ROWS // P
        NE = HEADS * D // P
        x = sb("fx", [P, NB, DM], F32)
        x1 = sb("x1", [P, NB, DM], F32)
        xc = sb("fxc", [P, NB, DM], F32)
        sq = sb("fsq", [P, NB, DM], F32)
        st = sb("fst", [P, 4, NB], F32)
        res = sb("res", [P, NB, DM], F32)
        ident = sb("fident", [P, P], F32)
        wo = sb("wo", [P, NE, DM], F32)
        w = sb("w", [DM, 3, DM], F32)
        bias = sb("bias", [DM, 1], F32)
        attnT = sb("attnT", [P, 2, ROWS], F32)
        hT = sb("hT", [DM, 5, ROWS], F32)

        tr = ctx.enter_context(nc.psum_tensor("tr", [P, 4, 512], F32))
        acc = ctx.enter_context(nc.psum_tensor("acc", [P, 2, 512], F32))

        s_in = sem("f_in")
        s_den = sem("f_den")
        s_norm = sem("f_norm")
        s_norm2 = sem("f_norm2")
        s_tr = sem("f_tr")
        s_ev = sem("f_ev")
        s_ev2 = sem("f_ev2")
        s_acc = sem("f_acc")
        s_t = sem("f_t")
        s_y = sem("f_y")
        s_mm = sem("f_mm")
        s_ln = sem("f_ln")
        s_sqrt = sem("f_sqrt")
        s_x1 = sem("f_x1")
        s_res = sem("f_res")
        s_out = sem("f_out")

        block = ctx.enter_context(nc.Block())

        def tr_bank(i):
            return tr[:, i % 4, :]

        def normalise(eng, e, done):
            cols = attn[:, :, e * P:(e + 1) * P].rearrange("p r (h n) -> p r h n", h=2)
            eng.tensor_tensor(cols, cols, den[:, :, 2 * e:2 * e + 2].unsqueeze(3).to_broadcast([P, NB, 2, D]),
                              ALU.mult).then_inc(done, 1)

        @block.gpsimd
        def _(pool):
            pool.wait_ge(s_den, 1)
            for e in range(1, NE, 2):
                normalise(pool, e, s_norm2)

        @block.sync
        def _(sp):
            sp.dma_start(ident[:, :], ins["ident"]).then_inc(s_in, 16)
            sp.dma_start(wo[:, :, :], ins["wo"]).then_inc(s_in, 16)
            sp.dma_start(x[:, :, :], ins["x"]).then_inc(s_in, 16)
            sp.dma_start(w[:, :, :], ins["w"]).then_inc(s_in, 16)
            sp.dma_start(bias[:, :], ins["bias"]).then_inc(s_in, 16)
            for half in range(2):
                sp.wait_ge(s_res, half + 1)
                sp.dma_start(out[:, half * 4:(half + 1) * 4, :], res[:, half * 4:(half + 1) * 4, :]
                             ).then_inc(s_out, 16)
            sp.wait_ge(s_out, 32)

        @block.tensor
        def _(pe):
            pe.wait_ge(s_in, 80)
            for e in range(NE + 1):
                if e < NE:
                    pe.wait_ge((s_norm, s_norm2)[e % 2], e // 2 + 1)
                    for half in range(2):
                        if e >= 2:
                            pe.wait_ge(s_ev if half == 0 else s_ev2, e - 1)
                        for q in range(4):
                            mm = pe.transpose(tr[:, (2 * e + half) % 4, q * P:(q + 1) * P],
                                              attn[:, half * 4 + q, e * P:(e + 1) * P], ident[:, :])
                        mm.then_inc(s_tr, 1)
                if e >= 1:
                    pe.wait_ge(s_ev, e)
                    pe.wait_ge(s_ev2, e)
                    for half in range(2):
                        mm = pe.matmul(acc[:, half, :], wo[:, e - 1, :],
                                       attnT[:, (e - 1) % 2, half * 512:(half + 1) * 512],
                                       start=(e == 1), stop=(e == NE))
                    mm.then_inc(s_acc, 1)
            for half in range(2):
                pe.wait_ge(s_t, half + 1)
                for q in range(4):
                    mm = pe.transpose(tr[:, half, q * P:(q + 1) * P],
                                      hT[:, 0, (half * 4 + q) * P:(half * 4 + q + 1) * P], ident[:, :])
                mm.then_inc(s_tr, 1)
            pe.wait_ge(s_ln, 9)
            for half in range(2):
                for q in range(4):
                    mm = pe.transpose(tr[:, 2 + half, q * P:(q + 1) * P], xc[:, half * 4 + q, :], ident[:, :])
                mm.then_inc(s_tr, 1)
            for i in range(3):
                for half in range(2):
                    pe.wait_ge(s_t, 2 + 2 * i + half + 1)
                    pe.matmul(acc[:, half, :], w[:, i, :], hT[:, 1 + i, half * 512:(half + 1) * 512],
                              start=True, stop=True).then_inc(s_mm, 1)
            for half in range(2):
                pe.wait_ge(s_y, half + 1)
                for q in range(4):
                    mm = pe.transpose(tr[:, half, q * P:(q + 1) * P],
                                      hT[:, 4, (half * 4 + q) * P:(half * 4 + q + 1) * P], ident[:, :])
                mm.then_inc(s_tr, 1)

        @block.vector
        def _(dve):
            dve.reciprocal(den[:, :, :], den[:, :, :]).then_inc(s_den, 1)
            dve.wait_ge(s_den, 1)
            normalise(dve, 0, s_norm)
            dve.wait_ge(s_in, 80)
            for e in range(NE):
                if e % 2 == 0 and e + 2 < NE:
                    normalise(dve, e + 2, s_norm)
                dve.wait_ge(s_tr, 2 * e + 1)
                if e >= 2:
                    dve.wait_ge(s_acc, e - 1)
                dve.tensor_copy(attnT[:, e % 2, 0:512], tr[:, (2 * e) % 4, :]).then_inc(s_ev, 1)
            for half in range(2):
                dve.wait_ge(s_acc, NE)
                dve.tensor_copy(hT[:, 0, half * 512:(half + 1) * 512], acc[:, half, :]).then_inc(s_t, 1)
            for half in range(2):
                dve.wait_ge(s_tr, 2 * NE + half + 1)
                rows = slice(half * 4, half * 4 + 4)
                dve.tensor_tensor(x1[:, rows, :], tr[:, half, :].rearrange("p (q n) -> p q n", q=4), x[:, rows, :],
                                  ALU.add).then_inc(s_x1, 1)
            dve.wait_ge(s_x1, 2)
            layer_norm(dve, None, x1[:, :, :], xc[:, :, :], sq[:, :, :], st, s_ln, s_sqrt, 0, 0, 1.0, "dve")
            for half in range(2):
                dve.wait_ge(s_tr, 2 * NE + 2 + half + 1)
                dve.tensor_copy(hT[:, 1, half * 512:(half + 1) * 512], tr[:, 2 + half, :]).then_inc(s_t, 1)
            for i in range(2):
                for half in range(2):
                    dve.wait_ge(s_mm, 2 * i + half + 1)
                    dve.tensor_copy(hT[:, 2 + i, half * 512:(half + 1) * 512], acc[:, half, :]).then_inc(s_t, 1)
            for half in range(2):
                dve.wait_ge(s_tr, 2 * NE + 4 + half + 1)
                rows = slice(half * 4, half * 4 + 4)
                dve.tensor_tensor(res[:, rows, :], tr[:, half, :].rearrange("p (q n) -> p q n", q=4),
                                  x1[:, rows, :], ALU.add).then_inc(s_res, 1)

        @block.scalar
        def _(act):
            for e in range(NE):
                act.wait_ge(s_tr, 2 * e + 2)
                if e >= 2:
                    act.wait_ge(s_acc, e - 1)
                act.copy(attnT[:, e % 2, 512:1024], tr[:, (2 * e + 1) % 4, :]).then_inc(s_ev2, 1)
            layer_norm(None, act, x1[:, :, :], xc[:, :, :], sq[:, :, :], st, s_ln, s_sqrt, 0, 0, 1.0, "act")
            for half in range(2):
                act.wait_ge(s_mm, 4 + half + 1)
                act.activation(hT[:, 4, half * 512:(half + 1) * 512], acc[:, half, :], ACT.Tanh,
                               bias=bias[:, 0:1]).then_inc(s_y, 1)


def build(nc, aps):
    ins = dict(aps)
    ext = aps["bias_ext"]

    def bias_rows(h):
        row = ext[bass.ds(h, 1), 0:TABLE]
        return overlapped(row)

    def overlapped(row):
        return bass.AP(row.tensor, row.offset, [[1, P], [1, TABLE]])

    ins["bias_rows"] = bias_rows
    attention(nc, ins, aps["out"])


def kernel(x, ctx_1024, mask_BxS2_bf1, L0_xattn_Wq, L0_xattn_Wk, L0_xattn_Wv, L0_xattn_Wo,
           L0_xattn_rel_pos_bias, L0_ffn_weight, L0_ffn_aux_weight1, L0_ffn_aux_weight2, L0_ffn_bias):
    import numpy as np
    import concourse.bacc as bacc
    from concourse.bass_utils import run_bass_kernel_spmd

    f32 = np.float32

    xr = np.asarray(x)[0, ::-1].reshape(ROWS // P, P, DM).transpose(1, 0, 2)
    ctxT = np.zeros((DM, KEYS_PAD), f32)
    ctxT[:, :KEYS] = np.asarray(ctx_1024)[0].T
    mask = np.zeros((KEYS_PAD,), bool)
    mask[:KEYS] = np.asarray(mask_BxS2_bf1)[0]
    mask_col = mask.reshape(-1, P).T

    expo = (np.arange(0, D, 2, dtype=f32) / f32(D)).astype(np.float64)
    inv = (f32(1) / (10000.0 ** expo).astype(f32)).astype(f32)
    inv = np.repeat(inv, 2)[None, :]
    sign = np.where(np.arange(D) < D // 2, -1.0, 1.0).astype(f32)

    def rotary(fn, positions):
        angle = (inv * positions.astype(f32)[:, None]).astype(np.float64)
        return fn(angle).astype(f32).reshape(-1, P, D).transpose(1, 0, 2)

    ext = np.abs(np.arange(TABLE + P) - (ROWS - 1)).clip(0, CLIP)
    bias_ext = np.asarray(L0_xattn_rel_pos_bias)[:, ext]
    row_const = np.zeros((P, 3), f32)
    row_const[ROW_PEN, 0], row_const[ROW_PEN, 1] = PEN, -PEN
    row_const[[ROW_NEGMAX_HI, ROW_NEGMAX_LO], 1] = 1.0
    row_const[ROW_PEN, 2] = 1.0
    arrays = {
        "x": xr, "ctxT": ctxT, "mask_row": mask[None, :], "mask_col": mask_col,
        "wq": np.asarray(L0_xattn_Wq), "wk": np.asarray(L0_xattn_Wk), "wv": np.asarray(L0_xattn_Wv),
        "wo": np.asarray(L0_xattn_Wo).reshape(-1, P, DM).transpose(1, 0, 2),
        "w": np.stack([np.asarray(a) for a in (L0_ffn_weight, L0_ffn_aux_weight1, L0_ffn_aux_weight2)], axis=1),
        "bias": np.asarray(L0_ffn_bias)[:, None],
        "bias_ext": bias_ext, "last_bias": np.asarray(L0_xattn_rel_pos_bias)[:, CLIP][None, :],
        "cos_k": rotary(np.cos, np.arange(KEYS_PAD)), "sin_k": sign * rotary(np.sin, np.arange(KEYS_PAD)),
        "cos_q": rotary(np.cos, np.arange(ROWS)[::-1]), "sin_q": sign * rotary(np.sin, np.arange(ROWS)[::-1]),
        "valid": (np.arange(KEYS_PAD).reshape(-1, P).T[:, -PAD_TILES:] < KEYS).astype(f32),
        "ident": np.eye(P, dtype=f32), "row_const": row_const,
    }
    arrays = {"in_" + k: np.ascontiguousarray(v) for k, v in arrays.items()}
    nc = bacc.Bacc("TRN2", target_bir_lowering=False, num_devices=1)
    aps = {k[3:]: nc.dram_tensor(k, v.shape, mybir.dt.from_np(v.dtype), kind="ExternalInput").ap()
           for k, v in arrays.items()}
    aps["out"] = nc.dram_tensor("out", (P, ROWS // P, DM), F32, kind="ExternalOutput").ap()
    build(nc, aps)
    got = run_bass_kernel_spmd(nc, [arrays], core_ids=[0]).results[0]["out"]
    return np.ascontiguousarray(got.transpose(1, 0, 2).reshape(ROWS, DM)[::-1])[None]
```
